# Optimizing a Trainium2 kernel written in Bass

```python
import numpy as np
import jax
import jax.numpy as jnp

def _softmax(x, axis=-1):
    return jax.nn.softmax(x, axis=axis)

def _gelu(x):
    return jax.nn.gelu(x, approximate=True)

def _silu(x):
    return jax.nn.silu(x)

def _sigmoid(x):
    return jax.nn.sigmoid(x)

def _layernorm(x, axis=-1, eps=1e-05):
    m = jnp.mean(x, axis=axis, keepdims=True)
    v = jnp.var(x, axis=axis, keepdims=True)
    return (x - m) / jnp.sqrt(v + eps)

def _scatter_add(tgt, idx, src, axis=0):
    return tgt.at[idx].add(src)

def _segment_sum(src, seg, n):
    return jax.ops.segment_sum(src, seg, n)
kernel_name = 'mk_gnn_resnorm_d4_gnn_r32_81050b'

def setup_inputs(seed: int=0):
    np.random.seed(seed)
    _w = jnp.asarray

    def _rec_inputs():
        import jax
        import jax.numpy as jnp
        _gk = jax.random.key(seed)
        x = -0.000202 + 1 * jax.random.normal(jax.random.fold_in(_gk, 1), (3125, 64), jnp.float32)
        src = jax.random.randint(jax.random.fold_in(_gk, 2), (100000,), 0, 3125, jnp.int32)
        dst = jax.random.randint(jax.random.fold_in(_gk, 3), (100000,), 0, 3125, jnp.int32)
        _o = jnp.argsort(dst, stable=True)
        src = src[_o]
        dst = dst[_o]
        edge_attr_32 = 0.000196303 + 1.00016 * jax.random.normal(jax.random.fold_in(_gk, 12), (100000, 32), jnp.float32)
        edge_attr_64 = -8.513e-05 + 0.999844 * jax.random.normal(jax.random.fold_in(_gk, 13), (100000, 64), jnp.float32)
        return (x, src, dst, edge_attr_32, edge_attr_64)
    x, src, dst, edge_attr_32, edge_attr_64 = _rec_inputs()

    def _L0_gnn_setup():
        import jax, jax.numpy as jnp
        import numpy as np
        N, D, E, ED, L = (3125, 64, 25000, 32, 5)
        LN_EPS = 1e-05

        def _leaky(x):
            return jax.nn.leaky_relu(x, negative_slope=0.1)
        key = jax.random.key(seed)
        ks = jax.random.split(key, 16)
        s = 0.05
        return {'x': jax.random.normal(ks[0], (N, D), dtype=jnp.float32), 'edge_index': jax.random.randint(ks[1], (2, E), 0, N, dtype=jnp.int64), 'edge_attr': jax.random.normal(ks[2], (E, ED), dtype=jnp.float32), 'W1': jax.random.normal(ks[3], (L, D, 2 * D), dtype=jnp.float32) * s, 'b1': jnp.zeros((L, 2 * D), dtype=jnp.float32), 'W2': jax.random.normal(ks[4], (L, 2 * D, D), dtype=jnp.float32) * s, 'b2': jnp.zeros((L, D), dtype=jnp.float32), 'We1': jax.random.normal(ks[5], (L, ED, D), dtype=jnp.float32) * s, 'be1': jnp.zeros((L, D), dtype=jnp.float32), 'We2': jax.random.normal(ks[6], (L, D, D), dtype=jnp.float32) * s, 'be2': jnp.zeros((L, D), dtype=jnp.float32), 'res_w': jnp.ones((L,), dtype=jnp.float32), 'dot_scale': jnp.ones((L,), dtype=jnp.float32), 'ln_g': jnp.ones((L, D), dtype=jnp.float32), 'ln_b': jnp.zeros((L, D), dtype=jnp.float32)}
    _L0_gnn_all = _L0_gnn_setup()
    _L0_gnn_in = {k: v for k, v in _L0_gnn_all.items() if k in ('W1', 'b1', 'W2', 'b2', 'We1', 'be1', 'We2', 'be2', 'res_w', 'dot_scale', 'ln_g', 'ln_b')}
    del _L0_gnn_all

    def _L1_gnn_setup():
        import jax, jax.numpy as jnp
        import numpy as np
        N_NODES = 3125
        N_EDGES = 1250000
        D_IN = 64
        D_OUT = 64
        key = jax.random.key(seed)
        k1, k2, k3, k4 = jax.random.split(key, 4)
        features = jax.random.normal(k1, (N_NODES, D_IN), dtype=jnp.float32)
        limit = float(np.sqrt(6.0 / (D_IN + D_OUT)))
        weight = jax.random.uniform(k2, (D_IN, D_OUT), minval=-limit, maxval=limit, dtype=jnp.float32)
        bias = jnp.zeros((D_OUT,), dtype=jnp.float32)
        src = jax.random.randint(k3, (N_EDGES,), 0, N_NODES, dtype=jnp.int32)
        dst = jax.random.randint(k4, (N_EDGES,), 0, N_NODES, dtype=jnp.int32)
        return {'features': features, 'weight': weight, 'bias': bias, 'src': src, 'dst': dst, 'n_nodes': N_NODES}
    _L1_gnn_all = _L1_gnn_setup()
    _L1_gnn_in = {k: v for k, v in _L1_gnn_all.items() if k in ('weight', 'bias')}
    del _L1_gnn_all

    def _L2_gnn_setup():
        import jax, jax.numpy as jnp
        import numpy as np
        N, E, D, H, C = (50000, 25000, 64, 2, 64)

        def _transformer_conv(x, src, dst, wq, bq, wk, bk, wv, bv, ws, bs):
            n = x.shape[0]
            q = (x @ wq + bq).reshape(n, H, C)
            k = (x @ wk + bk).reshape(n, H, C)
            v = (x @ wv + bv).reshape(n, H, C)
            qi = q[dst]
            kj = k[src]
            vj = v[src]
            alpha = jnp.einsum('ehc,ehc->eh', qi, kj) / jnp.sqrt(jnp.asarray(C, x.dtype))
            amax = jax.ops.segment_max(alpha, dst, num_segments=n)
            amax = jnp.where(jnp.isfinite(amax), amax, 0.0)
            ex = jnp.exp(alpha - amax[dst])
            denom = jax.ops.segment_sum(ex, dst, num_segments=n)
            a = ex / (denom[dst] + 1e-16)
            out = jax.ops.segment_sum(a[:, :, None] * vj, dst, num_segments=n)
            out = out.mean(axis=1)
            return out + x @ ws + bs
        key = jax.random.key(seed)
        ks = jax.random.split(key, 20)
        x = jax.random.normal(ks[0], (N, D), dtype=jnp.float32)
        edge_index = jax.random.randint(ks[1], (2, E), 0, N, dtype=jnp.int64)
        s = 1.0 / np.sqrt(D)

        def lin(k, din, dout):
            return jax.random.uniform(k, (din, dout), jnp.float32, -s, s)
        inp = {'x': x, 'edge_index': edge_index}
        i = 2
        for l, din in ((1, D), (2, C)):
            for nm, dout in (('wq', H * C), ('wk', H * C), ('wv', H * C), ('ws', C)):
                inp[f'l{l}_{nm}'] = lin(ks[i], din, dout)
                i += 1
                inp[f"l{l}_{nm.replace('w', 'b')}"] = jnp.zeros((dout,), jnp.float32)
        return inp
    _L2_gnn_all = _L2_gnn_setup()
    _L2_gnn_in = {k: v for k, v in _L2_gnn_all.items() if k in ('l1_wq', 'l1_bq', 'l1_wk', 'l1_bk', 'l1_wv', 'l1_bv', 'l1_ws', 'l1_bs', 'l2_wq', 'l2_bq', 'l2_wk', 'l2_bk', 'l2_wv', 'l2_bv', 'l2_ws', 'l2_bs')}
    del _L2_gnn_all

    def _L3_gnn_setup():
        import jax, jax.numpy as jnp
        import numpy as np
        N_NODES = 3125
        N_EDGES = 40000
        D_FEAT = 64
        EPS = 0.0
        key = jax.random.key(seed)
        k1, k2, k3, k4 = jax.random.split(key, 4)
        return {'node_inputs': jax.random.normal(k1, (N_NODES, D_FEAT), dtype=jnp.float32), 'edge_inputs': jax.random.normal(k2, (N_EDGES, D_FEAT), dtype=jnp.float32), 'src': jax.random.randint(k3, (N_EDGES,), 0, N_NODES, dtype=jnp.int32), 'dst': jax.random.randint(k4, (N_EDGES,), 0, N_NODES, dtype=jnp.int32)}
    _L3_gnn_all = _L3_gnn_setup()
    _L3_gnn_in = {k: v for k, v in _L3_gnn_all.items() if k in ()}
    del _L3_gnn_all
    return {'x': x, 'src': src, 'dst': dst, 'edge_attr_32': edge_attr_32, 'edge_attr_64': edge_attr_64, 'L0_gnn_W1': _L0_gnn_in['W1'], 'L0_gnn_b1': _L0_gnn_in['b1'], 'L0_gnn_W2': _L0_gnn_in['W2'], 'L0_gnn_b2': _L0_gnn_in['b2'], 'L0_gnn_We1': _L0_gnn_in['We1'], 'L0_gnn_be1': _L0_gnn_in['be1'], 'L0_gnn_We2': _L0_gnn_in['We2'], 'L0_gnn_be2': _L0_gnn_in['be2'], 'L0_gnn_res_w': _L0_gnn_in['res_w'], 'L0_gnn_dot_scale': _L0_gnn_in['dot_scale'], 'L0_gnn_ln_g': _L0_gnn_in['ln_g'], 'L0_gnn_ln_b': _L0_gnn_in['ln_b'], 'L1_gnn_weight': _L1_gnn_in['weight'], 'L1_gnn_bias': _L1_gnn_in['bias'], 'L2_gnn_l1_wq': _L2_gnn_in['l1_wq'], 'L2_gnn_l1_bq': _L2_gnn_in['l1_bq'], 'L2_gnn_l1_wk': _L2_gnn_in['l1_wk'], 'L2_gnn_l1_bk': _L2_gnn_in['l1_bk'], 'L2_gnn_l1_wv': _L2_gnn_in['l1_wv'], 'L2_gnn_l1_bv': _L2_gnn_in['l1_bv'], 'L2_gnn_l1_ws': _L2_gnn_in['l1_ws'], 'L2_gnn_l1_bs': _L2_gnn_in['l1_bs'], 'L2_gnn_l2_wq': _L2_gnn_in['l2_wq'], 'L2_gnn_l2_bq': _L2_gnn_in['l2_bq'], 'L2_gnn_l2_wk': _L2_gnn_in['l2_wk'], 'L2_gnn_l2_bk': _L2_gnn_in['l2_bk'], 'L2_gnn_l2_wv': _L2_gnn_in['l2_wv'], 'L2_gnn_l2_bv': _L2_gnn_in['l2_bv'], 'L2_gnn_l2_ws': _L2_gnn_in['l2_ws'], 'L2_gnn_l2_bs': _L2_gnn_in['l2_bs']}

def reference(x, src, dst, edge_attr_32, edge_attr_64, L0_gnn_W1, L0_gnn_b1, L0_gnn_W2, L0_gnn_b2, L0_gnn_We1, L0_gnn_be1, L0_gnn_We2, L0_gnn_be2, L0_gnn_res_w, L0_gnn_dot_scale, L0_gnn_ln_g, L0_gnn_ln_b, L1_gnn_weight, L1_gnn_bias, L2_gnn_l1_wq, L2_gnn_l1_bq, L2_gnn_l1_wk, L2_gnn_l1_bk, L2_gnn_l1_wv, L2_gnn_l1_bv, L2_gnn_l1_ws, L2_gnn_l1_bs, L2_gnn_l2_wq, L2_gnn_l2_bq, L2_gnn_l2_wk, L2_gnn_l2_bk, L2_gnn_l2_wv, L2_gnn_l2_bv, L2_gnn_l2_ws, L2_gnn_l2_bs):
    import jax
    import jax.numpy as jnp

    def _L0_gnn_ref(x, edge_index, edge_attr, W1, b1, W2, b2, We1, be1, We2, be2, res_w, dot_scale, ln_g, ln_b):
        import jax, jax.numpy as jnp
        import numpy as np
        N, D, E, ED, L = (3125, 64, 25000, 32, 5)
        LN_EPS = 1e-05

        def _leaky(x):
            return jax.nn.leaky_relu(x, negative_slope=0.1)
        src, dst = (edge_index[0], edge_index[1])
        n = x.shape[0]
        for l in range(W1.shape[0]):
            h = _leaky(x @ W1[l] + b1[l]) @ W2[l] + b2[l]
            e = _leaky(edge_attr @ We1[l] + be1[l]) @ We2[l] + be2[l]
            msg = h[src] * e * dot_scale[l]
            agg = jax.ops.segment_sum(msg, dst, num_segments=n)
            out = x + agg * res_w[l]
            mu = jnp.mean(out, axis=-1, keepdims=True)
            var = jnp.mean(jnp.square(out - mu), axis=-1, keepdims=True)
            x = (out - mu) * jax.lax.rsqrt(var + LN_EPS) * ln_g[l] + ln_b[l]
        return x

    def _L1_gnn_ref(features, weight, bias, src, dst, n_nodes):
        import jax, jax.numpy as jnp
        import numpy as np
        N_NODES = 3125
        N_EDGES = 1250000
        D_IN = 64
        D_OUT = 64
        ones_e = jnp.ones(src.shape[0], dtype=features.dtype)
        deg_out = jnp.maximum(jax.ops.segment_sum(ones_e, src, num_segments=n_nodes), 1.0)
        deg_in = jnp.maximum(jax.ops.segment_sum(ones_e, dst, num_segments=n_nodes), 1.0)
        h = features * (deg_out ** (-0.5))[:, None] @ weight
        rst = jax.ops.segment_sum(h[src], dst, num_segments=n_nodes)
        rst = rst * (deg_in ** (-0.5))[:, None] + bias
        return rst

    def _L2_gnn_ref(x, edge_index, l1_wq, l1_bq, l1_wk, l1_bk, l1_wv, l1_bv, l1_ws, l1_bs, l2_wq, l2_bq, l2_wk, l2_bk, l2_wv, l2_bv, l2_ws, l2_bs):
        import jax, jax.numpy as jnp
        import numpy as np
        N, E, D, H, C = (50000, 25000, 64, 2, 64)

        def _transformer_conv(x, src, dst, wq, bq, wk, bk, wv, bv, ws, bs):
            n = x.shape[0]
            q = (x @ wq + bq).reshape(n, H, C)
            k = (x @ wk + bk).reshape(n, H, C)
            v = (x @ wv + bv).reshape(n, H, C)
            qi = q[dst]
            kj = k[src]
            vj = v[src]
            alpha = jnp.einsum('ehc,ehc->eh', qi, kj) / jnp.sqrt(jnp.asarray(C, x.dtype))
            amax = jax.ops.segment_max(alpha, dst, num_segments=n)
            amax = jnp.where(jnp.isfinite(amax), amax, 0.0)
            ex = jnp.exp(alpha - amax[dst])
            denom = jax.ops.segment_sum(ex, dst, num_segments=n)
            a = ex / (denom[dst] + 1e-16)
            out = jax.ops.segment_sum(a[:, :, None] * vj, dst, num_segments=n)
            out = out.mean(axis=1)
            return out + x @ ws + bs
        src, dst = (edge_index[0], edge_index[1])
        h = _transformer_conv(x, src, dst, l1_wq, l1_bq, l1_wk, l1_bk, l1_wv, l1_bv, l1_ws, l1_bs)
        h = _transformer_conv(h, src, dst, l2_wq, l2_bq, l2_wk, l2_bk, l2_wv, l2_bv, l2_ws, l2_bs)
        return h

    def _L3_gnn_ref(node_inputs, edge_inputs, src, dst):
        import jax, jax.numpy as jnp
        import numpy as np
        N_NODES = 3125
        N_EDGES = 40000
        D_FEAT = 64
        EPS = 0.0
        msgs = jax.nn.relu(node_inputs[src] + edge_inputs)
        agg = jax.ops.segment_sum(msgs, dst, num_segments=node_inputs.shape[0])
        return (1.0 + EPS) * node_inputs + agg
    edge_index = jnp.stack([src, dst])
    x = _layernorm(x + _L0_gnn_ref(x, edge_index, edge_attr_32, L0_gnn_W1, L0_gnn_b1, L0_gnn_W2, L0_gnn_b2, L0_gnn_We1, L0_gnn_be1, L0_gnn_We2, L0_gnn_be2, L0_gnn_res_w, L0_gnn_dot_scale, L0_gnn_ln_g, L0_gnn_ln_b), axis=-1)
    x = _layernorm(x + _L1_gnn_ref(x, L1_gnn_weight, L1_gnn_bias, src, dst, 3125), axis=-1)
    x = _layernorm(x + _L2_gnn_ref(x, edge_index, L2_gnn_l1_wq, L2_gnn_l1_bq, L2_gnn_l1_wk, L2_gnn_l1_bk, L2_gnn_l1_wv, L2_gnn_l1_bv, L2_gnn_l1_ws, L2_gnn_l1_bs, L2_gnn_l2_wq, L2_gnn_l2_bq, L2_gnn_l2_wk, L2_gnn_l2_bk, L2_gnn_l2_wv, L2_gnn_l2_bv, L2_gnn_l2_ws, L2_gnn_l2_bs), axis=-1)
    x = _layernorm(x + _L3_gnn_ref(x, edge_attr_64, src, dst), axis=-1)
    return x

_drawn_inputs = setup_inputs


def setup_inputs(seed=0):
    import zlib

    import numpy as np

    out = dict(_drawn_inputs(seed))
    spreads = {'L0_gnn_b1': (0.0, 0.1),
     'L0_gnn_b2': (0.0, 0.1),
     'L0_gnn_be1': (0.0, 0.1),
     'L0_gnn_be2': (0.0, 0.1),
     'L0_gnn_res_w': (1.0, 0.2),
     'L0_gnn_dot_scale': (1.0, 0.2),
     'L0_gnn_ln_g': (1.0, 0.2),
     'L0_gnn_ln_b': (0.0, 0.1),
     'L1_gnn_bias': (0.0, 0.1),
     'L2_gnn_l1_bq': (0.0, 0.8),
     'L2_gnn_l1_bk': (0.0, 0.8),
     'L2_gnn_l1_bv': (0.0, 0.1),
     'L2_gnn_l1_bs': (0.0, 0.1),
     'L2_gnn_l2_bq': (0.0, 0.8),
     'L2_gnn_l2_bk': (0.0, 0.8),
     'L2_gnn_l2_bv': (0.0, 0.1),
     'L2_gnn_l2_bs': (0.0, 0.1)}
    factors = {'edge_attr_32': 2.799,
     'L2_gnn_l1_wq': 8.0,
     'L2_gnn_l1_wk': 7.891,
     'L2_gnn_l2_wq': 8.0,
     'L2_gnn_l2_wk': 8.0}
    for name, (base, spread) in spreads.items():
        noise = np.random.default_rng([zlib.crc32(name.encode()), seed]).standard_normal(out[name].shape)
        drawn = base * np.exp(spread * noise) if base else spread * noise
        out[name] = jnp.asarray(drawn.astype(out[name].dtype))
    for name, factor in factors.items():
        out[name] = (out[name] * factor).astype(out[name].dtype)
    return out
```

```python
from contextlib import ExitStack

import concourse.bass as bass
from concourse import mybir

ALU = mybir.AluOpType
ACT = mybir.ActivationFunctionType
F32 = mybir.dt.float32
BF16 = mybir.dt.bfloat16
I32 = mybir.dt.int32
U32 = mybir.dt.uint32
AX_X = mybir.AxisListType.X

P = 128
N = 3125
D = 64
E = 100000
DA = 32
LAYERS = 5
HEADS = 2
W = -(-N // P)
NP = W * P
TAIL = N - (W - 1) * P
EP = 125
ET = E // EP
GROUP = 2 * P
NG = -(-(E // GROUP + W) // 8) * 8
SLOTS = NG * GROUP
NB = 2 * NG
NI = NG // 2
U = 4
TRIPS = NI // U
ROW = D + DA + 2
SRC_AT, DST_AT = D + DA, D + DA + 1
ST = 10
S_STEPS = ET // ST
IDX = NI + U
CH = 4
CHUNKS = [(a, min(a + CH, W)) for a in range(0, W, CH)]
NCH = len(CHUNKS)
HC = HEADS * D
AW = HC + HEADS
QKVS = 3 * HC + D
NPAD = 96
LN_EPS = 1e-5
FAR = -1e30
FILL = 32
BIGW = (NI + 1) * P


class Chain:

    def __init__(self, eng, sem, base=0):
        self.eng, self.sem, self.base, self.n = eng, sem, base, 0

    def __call__(self, ins):
        self.n += 1
        ins.then_inc(self.sem, 1)
        self.eng.wait_ge(self.sem, self.base + self.n)


def graph_kernel(nc, x_in, src_in, dst_in, a32_in, a64_in, w1_in, b1_in, w2_in, b2_in, we1_in, be1_in,
                 we2_in, be2_in, resw_in, dots_in, lng_in, lnb_in, gw_in, gb_in, conv_in, out):
    with ExitStack() as ctx:
        def sb(name, shape, dt=F32):
            return ctx.enter_context(nc.sbuf_tensor(name, shape, dt))

        def sem(name):
            return ctx.enter_context(nc.semaphore(name))

        def dram(name, shape, dt=F32):
            return nc.dram_tensor(name, shape, dt, kind="Internal").ap()

        rows = dram("rows", (SLOTS, ROW))
        htab = dram("htab", (NP, D))
        kvtab = dram("kvtab", (NP, 2 * HC))
        vslot = dram("vslot", (NI, P, 4 * HC))
        dstT = dram("dstT", (NB, P), F32)

        big = sb("big", [P, BIGW])
        x = sb("x", [P, W, D])
        x0 = sb("x0", [P, W, D])
        t1 = sb("t1", [P, W, D])
        t2 = sb("t2", [P, W, D])
        tab = sb("tab", [P, W, D])
        xT = sb("xT", [D, NP])
        srcidx = sb("srcidx", [P, NB + 4 * U], U32)
        dstl = sb("dstl", [P, NB])
        idx = sb("idx", [P, U, 4], U32)
        g = sb("g", [P, U, 4, D])
        oh = sb("oh", [P, 2, 4, P])
        msg = sb("msg", [P, 2, 4, D])
        eb = sb("eb", [P, 4, D])
        hb = sb("hb", [P, U * P])
        hid = sb("hid", [P, 512])
        iota = sb("iota", [P, P])
        iotap = sb("iotap", [P, 1])
        ident = sb("ident", [P, P])
        zero = sb("zero", [P, 512])
        win = sb("win", [1, NG], I32)
        deg = sb("deg", [P, 2, W])
        st = sb("st", [P, 8, W])
        w1 = sb("w1", [D, 2 * D])
        w2 = sb("w2", [2 * D, D])
        we1 = sb("we1", [P, 2, P])
        we2 = sb("we2", [P, P])
        cols = sb("cols", [P, 4])
        scale = sb("scale", [P, 1])
        rowb = sb("rowb", [P, 4, D])

        def carver():
            at = [0]

            def carve(*shape, dt=F32):
                n = 1
                for s in shape:
                    n *= s
                words = n // 2 if dt == BF16 else n
                v = big[:, at[0]:at[0] + words]
                at[0] += words
                assert at[0] <= BIGW
                if dt != F32:
                    v = v.bitcast(dt)
                if len(shape) == 2:
                    v = v.rearrange("p (a b) -> p a b", a=shape[0])
                if len(shape) == 3:
                    v = v.rearrange("p (a b c) -> p a b c", a=shape[0], b=shape[1])
                return v
            return carve

        carve = carver()
        src_i = carve(ET, dt=I32)
        dst_i = carve(ET, dt=I32)
        tmp_i = carve(ET, dt=I32)
        key = carve(4, ET)
        mask = carve(ET)
        scan = carve(ET)
        zrow = carve(ET)
        slotf = carve(ET)
        slot = carve(ET, dt=U32)
        cnt = carve(W)
        base = carve(W)
        grp = carve(3, W)
        grp_i = carve(W, dt=I32)
        wid = carve(W)
        tri = carve(P)
        ones = carve(P)
        gio = carve(NG)
        gacc = carve(NG)
        fill = carve(FILL * ROW)
        stage = carve(2, ST, ROW)
        sidx = carve(2, ST, dt=U32)
        low = [[carve(ST, P, dt=BF16) for _ in range(2)] for _ in range(2)]
        high = [[carve(ST, W + 1, dt=BF16) for _ in range(2)] for _ in range(2)]

        carve = carver()
        q = carve(W, HC)
        skip = carve(W, D)
        acc = carve(W, AW)
        kv = carve(U, 4, 2 * HC)
        ohT = carve(2, 512)
        far = carve(2, 512)
        prod = carve(8, D)
        al = carve(2, 8)
        alpha = carve(NI * 8)
        alT = carve(2, P)
        pick = carve(8, P)
        dbc = carve(U, 512)
        gmax = carve(2, 4)
        nmax = carve(W * HEADS + NPAD)
        wcat = carve(QKVS)
        bcat = carve(QKVS)
        vbuf = carve(U, 4 * HC)
        vm = carve(2, 4, AW)
        dif = carve(2, 8)
        ex = carve(2, 8)
        kvs = carve(2, CH, 2 * HC)
        den = carve(W, HEADS)

        carve = carver()
        a64 = carve(U, 4, D)
        sum3 = carve(2, 4, D)

        rowst = t1[:, :, :].rearrange("p w f -> p (w f)")[:, 0:U * 4 * ROW].rearrange("p (u c r) -> p u c r", u=U, c=4)
        turned = t2[:, :, :].rearrange("p w f -> p (w f)")

        pacc = ctx.enter_context(nc.psum_tensor("pacc", [P, 2048], F32))
        pA = ctx.enter_context(nc.psum_tensor("pA", [P, 512], F32))
        pB = ctx.enter_context(nc.psum_tensor("pB", [P, 512], F32))
        pC = ctx.enter_context(nc.psum_tensor("pC", [P, 512], F32))
        pD = ctx.enter_context(nc.psum_tensor("pD", [P, 512], F32))
        pT = [pC, pD]
        pAB = [pA, pB]
        pspread = pacc[:, 1024:2048]

        ended = sem("ended")
        const_ready = sem("const_ready")
        p_chain = sem("p_chain")
        x_loaded = sem("x_loaded")
        ids_loaded = sem("ids_loaded")
        filled = sem("filled")
        v_chain = sem("v_chain")
        w_chain = sem("w_chain")
        s_chain = sem("s_chain")
        counted = sem("counted")
        crossed = sem("crossed")
        stage_loaded = [sem(f"stage_loaded{r}") for r in range(2)]
        stage_ready = sem("stage_ready")
        degree_used = sem("degree_used")
        rows_sent = [sem(f"rows_sent{r}") for r in range(2)]
        row_loaded = [sem(f"row_loaded{r}") for r in range(U)]
        row_split = sem("row_split")
        row_turned = sem("row_turned")
        row_kept = sem("row_kept")
        dst_turned = sem("dst_turned")
        dst_copied = sem("dst_copied")
        dst_stored = sem("dst_stored")
        weights = sem("weights")
        w_free = sem("w_free")
        x_ready = sem("x_ready")
        n_turned = sem("n_turned")
        n_copied = sem("n_copied")
        n_up = sem("n_up")
        n_biased = sem("n_biased")
        n_act = sem("n_act")
        n_down = sem("n_down")
        tab_ready = sem("tab_ready")
        tab_stored = sem("tab_stored")
        idx_ready = sem("idx_ready")
        gathered = [sem(f"gathered{r}") for r in range(U)]
        e_up = sem("e_up")
        e_biased = sem("e_biased")
        e_act = sem("e_act")
        e_down = sem("e_down")
        e_chain = sem("e_chain")
        l_chain = sem("l_chain")
        msg_ready = sem("msg_ready")
        scattered = sem("scattered")
        summed = sem("summed")
        conv_loaded = sem("conv_loaded")
        c_down = sem("c_down")
        c_used = sem("c_used")
        kvs_ready = sem("kvs_ready")
        kvs_stored = [sem(f"kvs_stored{r}") for r in range(2)]
        dbc_loaded = [sem(f"dbc_loaded{r}") for r in range(U)]
        ohT_ready = sem("ohT_ready")
        far_ready = sem("far_ready")
        q_ready = sem("q_ready")
        c_chain = sem("c_chain")
        b_chain = sem("b_chain")
        al_ready = sem("al_ready")
        al_turned = sem("al_turned")
        al_copied = sem("al_copied")
        al_spread = sem("al_spread")
        v_stored = [sem(f"v_stored{r}") for r in range(U)]
        v_loaded = [sem(f"v_loaded{r}") for r in range(U)]
        m_ready = sem("m_ready")
        dif_ready = sem("dif_ready")
        ex_ready = sem("ex_ready")
        vm_ready = sem("vm_ready")
        sums_ready = sem("sums_ready")
        a_loaded = [sem(f"a_loaded{r}") for r in range(U)]
        sum_ready = sem("sum_ready")
        deg_ready = sem("deg_ready")
        var_ready = sem("var_ready")
        root_ready = sem("root_ready")
        final_ready = sem("final_ready")
        stored = sem("stored")

        block = ctx.enter_context(nc.Block())
        PHASES = ["sorted", "unpacked", "L0", "L1", "scores0", "sums0", "conv0", "scores1", "sums1", "conv1"]

        def barrier(eng, name):
            eng.drain().then_inc(ended, 1)
            eng.wait_ge(ended, 5 * (PHASES.index(name) + 1))

        def hold(eng):
            eng.nop(nofuse=True)

        def nodes(t):
            return t.rearrange("(w p) f -> p w f", p=P)

        def flat(t):
            return t.rearrange("p w f -> p (w f)")

        def row_of(v, w):
            return v.rearrange("(o f) -> o f", o=1).to_broadcast([P, w])

        conv = [conv_in[0:8], conv_in[8:16]]
        WEIGHT_DMAS = 16 + 1
        TURNS = [(a, min(a + P, NB)) for a in range(0, NB, P)]
        SCORES = [LAYERS + 1, LAYERS + 2]

        @block.sync
        def _(sp):
            sp.dma_start(src_i[0:EP, :], src_in.rearrange("(p t) -> p t", p=EP)).then_inc(ids_loaded, 16)
            sp.dma_start(dst_i[0:EP, :], dst_in.rearrange("(p t) -> p t", p=EP)).then_inc(ids_loaded, 16)
            sp.wait_ge(const_ready, 1)
            sp.dma_start(x[:, 0:W - 1, :], nodes(x_in[0:(W - 1) * P, :])).then_inc(x_loaded, 16)
            sp.dma_start(x[0:TAIL, W - 1, :], x_in[(W - 1) * P:N, :]).then_inc(x_loaded, 16)
            rows_f = rows.rearrange("(p a r) c -> p a (r c)", p=P, r=FILL)
            with sp.Fori(0, SLOTS // P // FILL) as a:
                sp.dma_start(rows_f[:, bass.ds(a, 1), :].rearrange("p o c -> p (o c)"), fill).then_inc(filled, 16)

            a64_v = a64_in.rearrange("(p t) f -> p t f", p=EP)
            a32_v = a32_in.rearrange("(p t) f -> p t f", p=EP)

            def load_stage(t, r):
                i = t * 2 + r
                sp.dma_start(stage[0:EP, r, :, 0:D], a64_v[:, bass.ds(i * ST, ST), :]).then_inc(stage_loaded[r], 16)
                sp.dma_start(stage[0:EP, r, :, D:D + DA], a32_v[:, bass.ds(i * ST, ST), :]).then_inc(stage_loaded[r], 16)

            for r in range(2):
                load_stage(0, r)
            with sp.Fori(1, S_STEPS // 2) as t:
                for r in range(2):
                    sp.wait_ge(rows_sent[r], t * (16 * ST))
                    load_stage(t, r)
            for r in range(2):
                sp.wait_ge(rows_sent[r], S_STEPS // 2 * 16 * ST)
            barrier(sp, "sorted")

            rows_v = rows.rearrange("(i k p b) r -> i p k b r", k=2, p=P, b=2)

            def load_rows(t, r):
                for k in range(2):
                    sp.dma_start(rowst[:, r, 2 * k:2 * k + 2, :],
                                 rows_v[bass.ds(t * U + r, 1), :, k].rearrange("i p b r -> (i p) b r")).then_inc(row_loaded[r], 16)

            for r in range(U):
                load_rows(0, r)
            with sp.Fori(1, TRIPS) as t:
                for r in range(U):
                    sp.wait_ge(row_split, t * U + (r + 1 - U))
                    sp.wait_ge(row_turned, t * U + (r + 1 - U))
                    load_rows(t, r)
            for k, (a, b) in enumerate(TURNS):
                sp.wait_ge(dst_copied, k + 1)
                sp.dma_start(dstT[a:b, :], turned[0:b - a, k * P:(k + 1) * P]).then_inc(dst_stored, 16)
            sp.wait_ge(dst_stored, 16 * len(TURNS))
            barrier(sp, "unpacked")

            with sp.Fori(0, LAYERS) as l:
                def layer(v):
                    v = v[bass.ds(l, 1)]
                    return v.rearrange("o a b -> (o a) b") if len(v.shape) == 3 else v

                sp.wait_ge(w_free, l + 1)
                sp.dma_start(w1[:, :], layer(w1_in)).then_inc(weights, 16)
                sp.dma_start(w2[:, :], layer(w2_in)).then_inc(weights, 16)
                for c in range(4):
                    sp.dma_start(we1[c * DA:(c + 1) * DA, c // 2, (c % 2) * D:(c % 2 + 1) * D], layer(we1_in)).then_inc(weights, 16)
                for c in range(2):
                    sp.dma_start(we2[c * D:(c + 1) * D, c * D:(c + 1) * D], layer(we2_in)).then_inc(weights, 16)
                    sp.dma_start(cols[c * D:(c + 1) * D, 1:2], layer(be1_in).rearrange("o (a u) -> (o a) u", u=1)).then_inc(weights, 16)
                sp.dma_start(cols[:, 0:1], layer(b1_in).rearrange("o (a u) -> (o a) u", u=1)).then_inc(weights, 16)
                for k, v in enumerate((resw_in, dots_in)):
                    sp.dma_start(cols[:, 2 + k:3 + k], layer(v).rearrange("(o u) -> o u", u=1).to_broadcast([P, 1])).then_inc(weights, 16)
                for k, v in enumerate((b2_in, be2_in, lng_in, lnb_in)):
                    sp.dma_start(rowb[:, k, :], layer(v).to_broadcast([P, D])).then_inc(weights, 16)
                sp.wait_ge(tab_ready, l * NCH + NCH)
                sp.dma_start(nodes(htab), tab[:, :, :]).then_inc(tab_stored, 16)
            barrier(sp, "L0")

            sp.dma_start(w1[:, 0:D], gw_in).then_inc(weights, 16)
            sp.dma_start(rowb[:, 0, :], row_of(gb_in, D)).then_inc(weights, 16)
            sp.wait_ge(tab_ready, (LAYERS + 1) * NCH)
            sp.dma_start(nodes(htab), tab[:, :, :]).then_inc(tab_stored, 16)
            barrier(sp, "L1")

            dst_v = dstT.rearrange("(i c) p -> i (c p)", c=4)

            def load_dst(t, r):
                sp.dma_start(dbc[:, r, :], dst_v[bass.ds(t * U + r, 1), :].to_broadcast([P, 512])).then_inc(dbc_loaded[r], 16)

            for n in range(2):
                for k in range(4):
                    w = HC if k < 3 else D
                    sp.dma_start(wcat[0:D, k * HC:k * HC + w], conv[n][2 * k]).then_inc(conv_loaded, 16)
                    sp.dma_start(bcat[:, k * HC:k * HC + w], row_of(conv[n][2 * k + 1], w)).then_inc(conv_loaded, 16)
                for k, (a, b) in enumerate(CHUNKS):
                    sp.wait_ge(kvs_ready, n * NCH + k + 1)
                    sp.dma_start(nodes(kvtab)[:, a:b, :], kvs[:, k % 2, 0:b - a, :]).then_inc(kvs_stored[k % 2], 16)

                def store_v(t, r):
                    sp.wait_ge(gathered[r], (t + SCORES[n] * TRIPS) * 64 + 64)
                    sp.dma_start(vslot[bass.ds(t * U + r, 1)].rearrange("i p (c f) -> (i p) c f", c=4),
                                 kv[:, r, :, HC:2 * HC]).then_inc(v_stored[r], 16)

                for r in range(U):
                    load_dst(0, r)
                with sp.Fori(1, TRIPS) as t:
                    for r in range(U):
                        sp.wait_ge(ohT_ready, t * U + (r + 1 - U + 2 * n * NI))
                        load_dst(t, r)
                        store_v(t - 1, r)
                for r in range(U):
                    store_v(TRIPS - 1, r)
                for r in range(U):
                    sp.wait_ge(v_stored[r], (n + 1) * TRIPS * 16)
                barrier(sp, f"scores{n}")

                def load_v(t, r):
                    sp.dma_start(vbuf[:, r, :], vslot[bass.ds(t * U + r, 1)].rearrange("i p f -> (i p) f")).then_inc(v_loaded[r], 16)

                for r in range(U):
                    load_dst(0, r)
                    load_v(0, r)
                with sp.Fori(1, TRIPS) as t:
                    for r in range(U):
                        sp.wait_ge(ohT_ready, t * U + (r + 1 - U + (2 * n + 1) * NI))
                        load_dst(t, r)
                        sp.wait_ge(vm_ready, t * U + (r + 1 - U + n * NI))
                        load_v(t, r)
                barrier(sp, f"sums{n}")
                barrier(sp, f"conv{n}")

            sp.dma_start(nodes(htab), x[:, :, :]).then_inc(tab_stored, 16)

            def load_a(t, r):
                for k in range(2):
                    sp.dma_start(a64[:, r, 2 * k:2 * k + 2, :],
                                 rows_v[bass.ds(t * U + r, 1), :, k, :, 0:D].rearrange("i p b r -> (i p) b r")).then_inc(a_loaded[r], 16)

            for r in range(U):
                load_a(0, r)
            with sp.Fori(1, TRIPS) as t:
                for r in range(U):
                    sp.wait_ge(sum_ready, t * U + (r + 1 - U))
                    load_a(t, r)
            sp.wait_ge(final_ready, 1)
            sp.dma_start(nodes(out[0:(W - 1) * P, :]), x[:, 0:W - 1, :]).then_inc(stored, 16)
            sp.dma_start(out[(W - 1) * P:N, :], x[0:TAIL, W - 1, :]).then_inc(stored, 16)
            sp.wait_ge(stored, 32)

        @block.gpsimd
        def _(pool):
            chain = Chain(pool, p_chain)
            pool.memset(x[:, W - 1, :], 0.0)
            chain(pool.memset(fill, 0.0))
            chain(pool.memset(fill.rearrange("p (r c) -> p r c", c=ROW)[:, :, DST_AT:DST_AT + 1], -1.0))
            pool.memset(zero[:, :], 0.0)
            pool.memset(ones, 1.0)
            pool.memset(we1[:, :, :], 0.0)
            pool.memset(we2[:, :], 0.0)
            pool.memset(ident[:, :], 0.0)
            chain(pool.memset(tri, 1.0))
            pool.iota(iota[:, :], pattern=[[1, P]], base=0, channel_multiplier=0, allow_small_or_imprecise_dtypes=True)
            pool.iota(iotap[:, :], pattern=[[0, 1]], base=0, channel_multiplier=1, allow_small_or_imprecise_dtypes=True)
            pool.iota(wid, pattern=[[1, W]], base=0, channel_multiplier=0, allow_small_or_imprecise_dtypes=True)
            pool.iota(gio, pattern=[[1, NG]], base=0, channel_multiplier=0, allow_small_or_imprecise_dtypes=True)
            pool.affine_select(out=ident[:, :], in_=ident[:, :], compare_op=ALU.not_equal, fill=1.0, base=0,
                               pattern=[[-1, P]], channel_multiplier=1)
            chain(pool.affine_select(out=tri, in_=tri, compare_op=ALU.is_gt, fill=0.0, base=0,
                                     pattern=[[1, P]], channel_multiplier=-1))
            pool.drain().then_inc(const_ready, 1)
            pool.wait_ge(filled, SLOTS // P // FILL * 16)

            with pool.Fori(0, S_STEPS // 2) as t:
                for r in range(2):
                    pool.wait_ge(stage_loaded[r], t * 32 + 32)
                    pool.wait_ge(stage_ready, t * 2 + (r + 1))
                    hold(pool)
                    for c in range(ST):
                        pool.indirect_dma_start(
                            out=rows[:, :], out_offset=bass.IndirectOffsetOnAxis(ap=sidx[0:EP, r, c:c + 1], axis=0),
                            in_=stage[0:EP, r, c, :], in_offset=None).then_inc(rows_sent[r], 16)
            barrier(pool, "sorted")
            barrier(pool, "unpacked")

            def gather(table, into, r):
                for c in range(4):
                    pool.indirect_dma_start(
                        out=into[:, r, c, :], out_offset=None, in_=table[:, :],
                        in_offset=bass.IndirectOffsetOnAxis(ap=idx[:, r, c:c + 1], axis=0)).then_inc(gathered[r], 16)

            with pool.Fori(0, LAYERS) as l:
                pool.wait_ge(tab_stored, l * 16 + 16)
                hold(pool)
                with pool.Fori(0, TRIPS) as t:
                    for r in range(U):
                        pool.wait_ge(idx_ready, l * IDX + t * U + (r + 1))
                        hold(pool)
                        gather(htab, g, r)
            barrier(pool, "L0")

            pool.wait_ge(tab_stored, LAYERS * 16 + 16)
            with pool.Fori(0, TRIPS) as t:
                for r in range(U):
                    pool.wait_ge(idx_ready, t * U + (LAYERS * IDX + r + 1))
                    pool.wait_ge(scattered, t * U + (LAYERS * NI + 2 + r + 1 - U))
                    hold(pool)
                    gather(htab, g, r)
            barrier(pool, "L1")

            pool.memset(pick, 0.0).then_inc(p_chain, 1)
            pool.wait_ge(p_chain, chain.n + 1)
            pool.affine_select(out=pick, in_=pick, compare_op=ALU.not_equal, fill=1.0, base=0,
                               pattern=[[-1, 8], [0, P]], channel_multiplier=1)
            pool.drain().then_inc(const_ready, 1)
            for n in range(2):
                for k in range(2):
                    pool.wait_ge(kvs_stored[k], 16 * (n + 1) * len(CHUNKS[k::2]))

                def step(t, r, first):
                    pool.wait_ge(idx_ready, t * U + (SCORES[n] * IDX + r + 1))
                    if not first:
                        pool.wait_ge(v_stored[r], t * 16 + n * TRIPS * 16)
                    hold(pool)
                    gather(kvtab, kv, r)

                for r in range(U):
                    step(0, r, True)
                with pool.Fori(1, TRIPS) as t:
                    for r in range(U):
                        step(t, r, False)
                barrier(pool, f"scores{n}")
                barrier(pool, f"sums{n}")
                barrier(pool, f"conv{n}")

            pool.wait_ge(tab_stored, (LAYERS + 2) * 16)
            with pool.Fori(0, TRIPS) as t:
                for r in range(U):
                    pool.wait_ge(idx_ready, t * U + ((LAYERS + 3) * IDX + r + 1))
                    hold(pool)
                    gather(htab, g, r)

        @block.scalar
        def _(act):
            act.drain().then_inc(row_kept, 2)

            def root(nth):
                act.wait_ge(var_ready, nth)
                act.activation(st[:, 4, :], st[:, 3, :], ACT.Sqrt).then_inc(root_ready, 1)

            act.wait_ge(deg_ready, 1)
            act.activation(deg[:, :, :], deg[:, :, :], ACT.Sqrt).then_inc(deg_ready, 1)
            barrier(act, "sorted")
            with act.Fori(0, TRIPS) as t:
                for r in range(U):
                    act.wait_ge(row_turned, t * U + (r + 1))
                    act.copy(big[:, bass.ds((t * U + r) * P, P)], pT[r % 2][:, 0:P]).then_inc(row_kept, 1)
            for k, (a, b) in enumerate(TURNS):
                act.wait_ge(dst_turned, k + 1)
                act.copy(turned[0:b - a, k * P:(k + 1) * P], pT[k % 2][0:b - a, 0:P]).then_inc(dst_copied, 1)
            barrier(act, "unpacked")

            def copy_turned(first):
                for k, (a, b) in enumerate(CHUNKS):
                    act.wait_ge(n_turned, first + (k + 1))
                    act.copy(xT[:, a * P:b * P], pT[k % 2][0:D, 0:(b - a) * P]).then_inc(n_copied, 1)

            with act.Fori(0, LAYERS) as l:
                copy_turned(l * NCH)
                act.wait_ge(weights, l * (16 * WEIGHT_DMAS) + 16 * WEIGHT_DMAS)
                for k, (a, b) in enumerate(CHUNKS):
                    act.wait_ge(n_up, l * NCH + (k + 1))
                    act.activation(hb[:, 0:(b - a) * P], pA[:, 0:(b - a) * P], ACT.Identity, bias=cols[:, 0:1]).then_inc(n_biased, 1)
                with act.Fori(0, TRIPS) as t:
                    for r in range(U):
                        act.wait_ge(e_up, l * (NI + 1) + t * U + (r + 1))
                        act.activation(hb[:, 0:2 * P], pA[:, 0:2 * P], ACT.Identity, bias=cols[:, 1:2]).then_inc(e_biased, 1)
                root(l + 1)
            root(LAYERS + 1)
            barrier(act, "L0")
            copy_turned(LAYERS * NCH)
            root(LAYERS + 2)
            barrier(act, "L1")
            for n in range(2):
                copy_turned((LAYERS + 1 + n) * NCH)

                def far_of(t, r, at):
                    act.wait_ge(ohT_ready, at)
                    act.activation(far[:, r % 2, :], ohT[:, r % 2, :], ACT.Copy, scale=-FAR, bias=FAR).then_inc(far_ready, 1)

                far_of(0, 0, 2 * n * NI + 1)

                def step(t, r, first, last):
                    act.wait_ge(al_ready, t * U + (r + 1 + n * NI))
                    act.copy(alpha[:, bass.ds((t * U + r) * 8, 8)], al[:, r % 2, :])
                    act.wait_ge(al_turned, t * U + (r + 1 + n * NI))
                    act.copy(alT[0:8, r % 2, :], pA[0:8, (r % 2) * P:(r % 2 + 1) * P]).then_inc(al_copied, 1)
                    if not last:
                        if not (first and r == 0):
                            act.wait_ge(c_chain, (t * U + (r + n * NI)) * 3)
                        far_of(t, r + 1, t * U + (r + 2 + 2 * n * NI))

                for r in range(U):
                    step(0, r, True, False)
                with act.Fori(1, TRIPS - 1) as t:
                    for r in range(U):
                        step(t, r, False, False)
                for r in range(U):
                    step(TRIPS - 1, r, False, r == U - 1)
                barrier(act, f"scores{n}")
                with act.Fori(0, TRIPS) as t:
                    for r in range(U):
                        act.wait_ge(dif_ready, t * U + (r + 1 + n * NI))
                        act.activation(ex[:, r % 2, :], dif[:, r % 2, :], ACT.Exp, scale=float(D) ** -0.5).then_inc(ex_ready, 1)
                barrier(act, f"sums{n}")
                if n == 1:
                    root(LAYERS + 3)
                barrier(act, f"conv{n}")
            with act.Fori(0, TRIPS) as t:
                for r in range(U):
                    act.wait_ge(sum_ready, t * U + (r + 1))
                    act.activation(msg[:, r % 2, :, :], sum3[:, r % 2, :, :], ACT.Relu).then_inc(msg_ready, 1)
            root(LAYERS + 4)

        @block.tensor
        def _(pe):
            pe.wait_ge(const_ready, 1)
            pe.wait_ge(counted, 1)
            pe.matmul(pA[:, 0:W], tri[0:EP, :], cnt[0:EP, :], start=True, stop=True)
            pe.matmul(pB[:, 0:W], ones[0:EP, :], cnt[0:EP, :], start=True, stop=True).then_inc(crossed, 1)
            for k in range(2):
                pe.matmul(pT[k][:, 0:W], zero[:, 0:P], zero[:, 0:W], start=True, stop=False, skip_group_check=True)
            with pe.Fori(0, S_STEPS // 2) as t:
                for r in range(2):
                    pe.wait_ge(stage_ready, t * 2 + (r + 1))
                    for k in range(2):
                        for c in range(ST):
                            last = pe.matmul(pT[k][:, 0:W], low[r][k][0:EP, c, :], high[r][k][0:EP, c, 0:W],
                                             start=False, stop=False, skip_group_check=True)
                    last.then_inc(degree_used, 1)
            barrier(pe, "sorted")
            with pe.Fori(0, TRIPS) as t:
                for r in range(U):
                    pe.wait_ge(row_split, t * U + (r + 1))
                    pe.wait_ge(row_kept, t * U + (r + 1))
                    pe.transpose(pT[r % 2][:, 0:P], hb[:, r * P:(r + 1) * P], ident[:, :]).then_inc(row_turned, 1)
            pe.wait_ge(row_kept, NI + 2)
            pe.wait_ge(row_split, NI)
            for k, (a, b) in enumerate(TURNS):
                if k >= 2:
                    pe.wait_ge(dst_copied, k - 1)
                pe.transpose(pT[k % 2][0:b - a, 0:P], dstl[:, a:b], ident[:, :]).then_inc(dst_turned, 1)
            pe.drain().then_inc(scattered, 2)
            barrier(pe, "unpacked")

            def turn(src, first):
                for k, (a, b) in enumerate(CHUNKS):
                    if k >= 2:
                        pe.wait_ge(n_copied, first + (k - 1))
                    hold(pe)
                    for w in range(a, b):
                        last = pe.transpose(pT[k % 2][0:D, (w - a) * P:(w - a + 1) * P], src[:, w, :], ident[:, :])
                    last.then_inc(n_turned, 1)

            def open_sums():
                for b in range(4):
                    pe.matmul(pacc[:, b * 512:(b + 1) * 512], zero[:, 0:P], zero[:, :], start=True, stop=False, skip_group_check=True)

            def scatter(i, r, rows_of):
                for k in range(2):
                    w = pe.value_load(win[0:1, bass.ds(i * 2 + k, 1)], min_val=0, max_val=W - 1)
                    for b in range(2):
                        c = 2 * k + b
                        last = pe.matmul(pacc[:, bass.ds(w * D, D)], oh[:, r % 2, c, :], rows_of(r, c),
                                         start=False, stop=False, skip_group_check=True)
                last.then_inc(scattered, 1)

            def up(i):
                for k in range(2):
                    last = pe.matmul(pA[:, k * P:(k + 1) * P], we1[:, k, :], big[:, bass.ds(i * P, P)], start=True, stop=True)
                last.then_inc(e_up, 1)

            with pe.Fori(0, LAYERS) as l:
                pe.wait_ge(x_ready, l + 1)
                turn(x, l * NCH)
                open_sums()
                pe.wait_ge(weights, l * (16 * WEIGHT_DMAS) + 16 * WEIGHT_DMAS)
                for k, (a, b) in enumerate(CHUNKS):
                    pe.wait_ge(n_copied, l * NCH + (k + 1))
                    pe.matmul(pA[:, 0:(b - a) * P], w1[:, :], xT[:, a * P:b * P], start=True, stop=True).then_inc(n_up, 1)
                    pe.wait_ge(n_act, l * NCH + (k + 1))
                    for w in range(b - a):
                        last = pe.matmul(pB[:, w * D:(w + 1) * D], hid[:, w * P:(w + 1) * P], w2[:, :], start=True, stop=True)
                    last.then_inc(n_down, 1)
                up(0)
                with pe.Fori(0, TRIPS) as t:
                    for r in range(U):
                        pe.wait_ge(e_act, l * NI + t * U + (r + 1))
                        for k in range(2):
                            last = pe.matmul(pB[:, k * P:(k + 1) * P], hid[:, k * P:(k + 1) * P], we2[:, :], start=True, stop=True)
                        last.then_inc(e_down, 1)
                        up(t * U + (r + 1))
                        pe.wait_ge(msg_ready, l * NI + t * U + (r + 1))
                        scatter(t * U + r, r, lambda r, c: msg[:, r % 2, c, :])
                pe.drain().then_inc(summed, 1)
            barrier(pe, "L0")

            pe.wait_ge(x_ready, LAYERS + 2)
            turn(t2, LAYERS * NCH)
            open_sums()
            pe.wait_ge(weights, LAYERS * 16 * WEIGHT_DMAS + 32)
            for k, (a, b) in enumerate(CHUNKS):
                pe.wait_ge(n_copied, LAYERS * NCH + k + 1)
                if k:
                    pe.wait_ge(tab_ready, LAYERS * NCH + k)
                for w in range(a, b):
                    last = pe.matmul(pB[:, (w - a) * D:(w - a + 1) * D], xT[:, w * P:(w + 1) * P], w1[:, 0:D], start=True, stop=True)
                last.then_inc(n_down, 1)
            with pe.Fori(0, TRIPS) as t:
                for r in range(U):
                    pe.wait_ge(gathered[r], t * 64 + (LAYERS * TRIPS * 64 + 64))
                    pe.wait_ge(msg_ready, t * U + (LAYERS * NI + r + 1))
                    scatter(t * U + r, r, lambda r, c: g[:, r, c, :])
            pe.drain().then_inc(summed, 1)
            barrier(pe, "L1")

            pe.wait_ge(const_ready, 2)
            for n in range(2):
                turn((x, x0)[n], (LAYERS + 1 + n) * NCH)
                pe.wait_ge(conv_loaded, 128 * (n + 1))
                for k, (a, b) in enumerate(CHUNKS):
                    pe.wait_ge(n_copied, (LAYERS + 1 + n) * NCH + k + 1)
                    for w in range(a, b):
                        if w >= 2:
                            pe.wait_ge(c_used, n * W + w - 1)
                        pe.matmul(pAB[w % 2][:, 0:QKVS], xT[:, w * P:(w + 1) * P], wcat[0:D, :], start=True, stop=True).then_inc(c_down, 1)
                pe.wait_ge(c_used, (n + 1) * W)

                def spread(t, r, at, first):
                    pe.wait_ge(al_copied, at)
                    if not first:
                        pe.wait_ge(c_chain, (at - 1) * 3)
                    for c in range(4):
                        for h in range(HEADS):
                            col = ((c // 2) * 4 + h * 2 + c % 2) * P
                            last = pe.matmul(pspread[:, col:col + P], pick[0:8, 2 * c + h, :], alT[0:8, r % 2, :], start=True, stop=True)
                    last.then_inc(al_spread, 1)

                def step(t, r, first):
                    pe.wait_ge(ohT_ready, t * U + (r + 1 + 2 * n * NI))
                    for k in range(2):
                        w = pe.value_load(win[0:1, bass.ds((t * U + r) * 2 + k, 1)], min_val=0, max_val=W - 1)
                        for b in range(2):
                            c = 2 * k + b
                            last = pe.matmul(pacc[:, (r % 2) * 512 + c * P:(r % 2) * 512 + (c + 1) * P],
                                             ohT[:, r % 2, c * P:(c + 1) * P], flat(q)[:, bass.ds(w * HC, HC)], start=True, stop=True)
                    last.then_inc(q_ready, 1)
                    if not (first and r == 0):
                        spread(t, r - 1, t * U + (r + n * NI), first and r == 1)
                    pe.wait_ge(al_ready, t * U + (r + 1 + n * NI))
                    pe.transpose(pA[0:8, (r % 2) * P:(r % 2 + 1) * P], al[:, r % 2, :], ident[:, :]).then_inc(al_turned, 1)

                for r in range(U):
                    step(0, r, True)
                with pe.Fori(1, TRIPS) as t:
                    for r in range(U):
                        step(t, r, False)
                spread(TRIPS - 1, U - 1, (n + 1) * NI, False)
                barrier(pe, f"scores{n}")

                with pe.Fori(0, TRIPS) as t:
                    for r in range(U):
                        pe.wait_ge(ohT_ready, t * U + (r + 1 + (2 * n + 1) * NI))
                        for k in range(2):
                            w = pe.value_load(win[0:1, bass.ds((t * U + r) * 2 + k, 1)], min_val=0, max_val=W - 1)
                            for b in range(2):
                                c = 2 * k + b
                                last = pe.matmul(pacc[:, (r % 2) * 512 + c * NPAD:(r % 2) * 512 + (c + 1) * NPAD],
                                                 ohT[:, r % 2, c * P:(c + 1) * P], nmax[:, bass.ds(w * HEADS, NPAD)], start=True, stop=True)
                        last.then_inc(m_ready, 1)
                        pe.wait_ge(vm_ready, t * U + (r + 1 + n * NI))
                        for c in range(4):
                            last = pe.matmul(pAB[r % 2][:, (c // 2) * AW:(c // 2 + 1) * AW], oh[:, r % 2, c, :],
                                             vm[:, r % 2, c, :], start=(c % 2 == 0), stop=(c % 2 == 1))
                        last.then_inc(sums_ready, 1)
                barrier(pe, f"sums{n}")
                barrier(pe, f"conv{n}")

            open_sums()
            with pe.Fori(0, TRIPS) as t:
                for r in range(U):
                    pe.wait_ge(msg_ready, t * U + ((LAYERS + 1) * NI + r + 1))
                    scatter(t * U + r, r, lambda r, c: msg[:, r % 2, c, :])
            pe.drain().then_inc(summed, 1)

        @block.vector
        def _(dve):
            chain = Chain(dve, v_chain)

            def over(v, n):
                return v.unsqueeze(2).to_broadcast([v.shape[0], v.shape[1], n])

            def each(v, n):
                return v.unsqueeze(1).to_broadcast([v.shape[0], n, v.shape[1]])

            dve.wait_ge(const_ready, 1)
            dve.wait_ge(ids_loaded, 32)
            for k, ids in enumerate((src_i, dst_i)):
                chain(dve.tensor_scalar(tmp_i[0:EP, :], ids[0:EP, :], P - 1, None, ALU.bitwise_and))
                chain(dve.tensor_copy(key[0:EP, 2 * k, :], tmp_i[0:EP, :]))
                chain(dve.tensor_scalar(tmp_i[0:EP, :], ids[0:EP, :], P.bit_length() - 1, None, ALU.logical_shift_right))
                chain(dve.tensor_copy(key[0:EP, 2 * k + 1, :], tmp_i[0:EP, :]))
            dve.memset(zrow, 0.0)
            chain(dve.memset(gacc, 0.0))

            with dve.Fori(0, W) as w:
                wc = Chain(dve, w_chain, w)
                wc(dve.tensor_scalar(mask[0:EP, :], key[0:EP, 3, :], wid[0:EP, bass.ds(w, 1)], 0.0, ALU.is_equal, ALU.add,
                                     accum_out=cnt[0:EP, bass.ds(w, 1)]))
            dve.drain().then_inc(counted, 1)
            dve.wait_ge(crossed, 1)
            chain(dve.tensor_scalar(grp[:, 0, :], pB[:, 0:W], float(GROUP - 1), None, ALU.add))
            chain(dve.tensor_copy(grp_i, grp[:, 0, :]))
            chain(dve.tensor_scalar(grp_i, grp_i, GROUP.bit_length() - 1, None, ALU.logical_shift_right))
            chain(dve.tensor_copy(grp[:, 0, :], grp_i))
            chain(dve.tensor_tensor_scan(grp[:, 1, :], grp[:, 0, :], zrow[:, 0:W], 0.0, ALU.add, ALU.add))
            chain(dve.tensor_tensor(grp[:, 2, :], grp[:, 1, :], grp[:, 0, :], ALU.subtract))
            chain(dve.scalar_tensor_tensor(base, grp[:, 2, :], float(GROUP), pA[:, 0:W], ALU.mult, ALU.add))
            chain(dve.tensor_scalar(base, base, -1.0, None, ALU.add))
            with dve.Fori(0, W) as w:
                sc = Chain(dve, s_chain, w * 4)
                sc(dve.tensor_scalar(mask[0:EP, :], key[0:EP, 3, :], wid[0:EP, bass.ds(w, 1)], None, ALU.is_equal))
                sc(dve.tensor_tensor_scan(scan[0:EP, :], mask[0:EP, :], zrow[0:EP, :], base[0:EP, bass.ds(w, 1)], ALU.add, ALU.add))
                hold(dve)
                sc(dve.copy_predicated(slotf[0:EP, :], mask[0:EP, :].bitcast(U32), scan[0:EP, :]))
                sc(dve.scalar_tensor_tensor(gacc, gio, grp[:, 1, bass.ds(w, 1)], gacc, ALU.is_ge, ALU.add))
            chain(dve.tensor_copy(slot[0:EP, :], slotf[0:EP, :]))
            chain(dve.tensor_scalar(gacc, gacc, float(W - 1), None, ALU.min))
            chain(dve.tensor_copy(win[0:1, :], gacc[0:1, :]))

            stage_i = stage.bitcast(I32)

            def stage_step(t, r, first):
                i = t * 2 + r
                if not first:
                    dve.wait_ge(rows_sent[r], t * (16 * ST))
                    dve.wait_ge(degree_used, t * 2 + (r - 1))
                dve.tensor_copy(sidx[0:EP, r, :], slot[0:EP, bass.ds(i * ST, ST)])
                dve.tensor_copy(stage_i[0:EP, r, :, SRC_AT], src_i[0:EP, bass.ds(i * ST, ST)])
                dve.tensor_copy(stage[0:EP, r, :, DST_AT], key[0:EP, 2, bass.ds(i * ST, ST)])
                for k in range(2):
                    dve.tensor_tensor(low[r][k][0:EP, :, :], each(iota[0:EP, :], ST), over(key[0:EP, 2 * k, bass.ds(i * ST, ST)], P), ALU.is_equal)
                    last = dve.tensor_tensor(high[r][k][0:EP, :, 0:W], each(wid[0:EP, :], ST),
                                             over(key[0:EP, 2 * k + 1, bass.ds(i * ST, ST)], W), ALU.is_equal)
                last.then_inc(stage_ready, 1)

            for r in range(2):
                stage_step(0, r, True)
            with dve.Fori(1, S_STEPS // 2) as t:
                for r in range(2):
                    stage_step(t, r, False)
            dve.wait_ge(degree_used, S_STEPS)
            for k in range(2):
                last = dve.tensor_scalar(deg[:, k, :], pT[k][:, 0:W], 1.0, None, ALU.max)
            last.then_inc(deg_ready, 1)
            dve.wait_ge(deg_ready, 2)
            chain(dve.reciprocal(deg[:, :, :], deg[:, :, :]))
            barrier(dve, "sorted")

            chain(dve.memset(srcidx[:, NB:], 0))
            rowst_u = rowst.bitcast(U32)
            with dve.Fori(0, TRIPS) as t:
                for r in range(U):
                    dve.wait_ge(row_loaded[r], t * 32 + 32)
                    dve.tensor_copy(hb[:, r * P:(r + 1) * P].rearrange("p (c f) -> p c f", c=4), rowst[:, r, :, D:D + DA])
                    dve.tensor_copy(srcidx[:, bass.ds((t * U + r) * 4, 4)], rowst_u[:, r, :, SRC_AT])
                    dve.tensor_copy(dstl[:, bass.ds((t * U + r) * 4, 4)], rowst[:, r, :, DST_AT]).then_inc(row_split, 1)
            dve.memset(big[:, NI * P:], 0.0)
            dve.wait_ge(x_loaded, 32)
            chain(dve.tensor_copy(x0[:, :, :], x[:, :, :]))
            barrier(dve, "unpacked")

            def copy_idx(i, r):
                dve.tensor_copy(idx[:, r, :], srcidx[:, bass.ds(i * 4, 4)]).then_inc(idx_ready, 1)

            def one_hot(i, r):
                return dve.tensor_tensor(oh[:, r % 2, :, :], each(iota[:, :], 4), over(dstl[:, bass.ds(i * 4, 4)], P), ALU.is_equal)

            def norm(ch, dst, affine, nth):
                ch(dve.tensor_reduce(st[:, 0, :], t1[:, :, :], AX_X, ALU.add))
                ch(dve.tensor_scalar(st[:, 1, :], st[:, 0, :], 1.0 / D, None, ALU.mult))
                ch(dve.tensor_tensor(t1[:, :, :], t1[:, :, :], over(st[:, 1, :], D), ALU.subtract))
                ch(dve.tensor_tensor(t2[:, :, :], t1[:, :, :], t1[:, :, :], ALU.mult))
                ch(dve.tensor_reduce(st[:, 2, :], t2[:, :, :], AX_X, ALU.add))
                dve.tensor_scalar(st[:, 3, :], st[:, 2, :], 1.0 / D, LN_EPS, ALU.mult, ALU.add).then_inc(var_ready, 1)
                dve.wait_ge(root_ready, nth)
                ch(dve.reciprocal(st[:, 5, :], st[:, 4, :]))
                ch(dve.tensor_tensor(dst[:, :, :], t1[:, :, :], over(st[:, 5, :], D), ALU.mult))
                if affine:
                    ch(dve.tensor_tensor(dst[:, :, :], dst[:, :, :], each(rowb[:, 2, :], W), ALU.mult))
                    ch(dve.tensor_tensor(dst[:, :, :], dst[:, :, :], each(rowb[:, 3, :], W), ALU.add))

            sums = pacc[:, 0:W * D]

            dve.drain().then_inc(x_ready, 1)
            dve.drain().then_inc(w_free, 1)
            END = 11
            with dve.Fori(0, LAYERS) as l:
                dve.wait_ge(weights, l * (16 * WEIGHT_DMAS) + 16 * WEIGHT_DMAS)
                for k, (a, b) in enumerate(CHUNKS):
                    n = (b - a) * P
                    dve.wait_ge(n_biased, l * NCH + (k + 1))
                    dve.scalar_tensor_tensor(hid[:, 0:n], hb[:, 0:n], 0.1, hb[:, 0:n], ALU.mult, ALU.max).then_inc(n_act, 1)
                    dve.wait_ge(n_down, l * NCH + (k + 1))
                    dve.tensor_tensor(tab[:, a:b, :], pB[:, 0:(b - a) * D].rearrange("p (w f) -> p w f", w=b - a),
                                      each(rowb[:, 0, :], b - a), ALU.add).then_inc(tab_ready, 1)
                for r in range(U):
                    copy_idx(r, r)
                with dve.Fori(0, TRIPS) as t:
                    for r in range(U):
                        i = t * U + r
                        dve.wait_ge(e_biased, l * NI + t * U + (r + 1))
                        dve.scalar_tensor_tensor(hid[:, 0:2 * P], hb[:, 0:2 * P], 0.1, hb[:, 0:2 * P], ALU.mult, ALU.max).then_inc(e_act, 1)
                        dve.wait_ge(scattered, l * NI + t * U + (r + 1))
                        one_hot(i, r)
                        dve.wait_ge(e_down, l * NI + t * U + (r + 1))
                        dve.tensor_tensor(eb[:, :, :], pB[:, 0:4 * D].rearrange("p (c f) -> p c f", c=4), each(rowb[:, 1, :], 4), ALU.add).then_inc(e_chain, 1)
                        dve.wait_ge(gathered[r], l * (TRIPS * 64) + t * 64 + 64)
                        dve.wait_ge(e_chain, l * NI + t * U + (r + 1))
                        dve.tensor_tensor(msg[:, r % 2, :, :], eb[:, :, :], g[:, r, :, :], ALU.mult).then_inc(msg_ready, 1)
                        copy_idx(i + U, r)
                lc = Chain(dve, l_chain, l * END)
                lc(dve.tensor_tensor(scale[:, :], cols[:, 2:3], cols[:, 3:4], ALU.mult))
                dve.wait_ge(summed, l + 1)
                lc(dve.scalar_tensor_tensor(flat(t1[:, :, :]), sums, scale[:, 0:1], flat(x[:, :, :]), ALU.mult, ALU.add))
                norm(lc, x, True, l + 1)
                assert lc.n == END
                hold(dve)
                dve.drain().then_inc(x_ready, 1)
                dve.drain().then_inc(w_free, 1)
            chain(dve.tensor_tensor(t1[:, :, :], x0[:, :, :], x[:, :, :], ALU.add))
            norm(chain, x, False, LAYERS + 1)
            barrier(dve, "L0")

            chain(dve.tensor_tensor(t2[:, :, :], x[:, :, :], over(deg[:, 0, :], D), ALU.mult))
            dve.drain().then_inc(x_ready, 1)
            for r in range(U):
                copy_idx(r, r)
            for k, (a, b) in enumerate(CHUNKS):
                dve.wait_ge(n_down, LAYERS * NCH + k + 1)
                dve.tensor_copy(flat(tab[:, a:b, :]), pB[:, 0:(b - a) * D]).then_inc(tab_ready, 1)
            with dve.Fori(0, TRIPS) as t:
                for r in range(U):
                    dve.wait_ge(scattered, t * U + (LAYERS * NI + r + 1))
                    one_hot(t * U + r, r).then_inc(msg_ready, 1)
                    dve.wait_ge(gathered[r], t * 64 + (LAYERS * TRIPS * 64 + 64))
                    copy_idx(t * U + (r + U), r)
            dve.wait_ge(summed, LAYERS + 1)
            dve.wait_ge(weights, LAYERS * 16 * WEIGHT_DMAS + 32)
            chain(dve.tensor_tensor(t1[:, :, :], sums.rearrange("p (w f) -> p w f", w=W), over(deg[:, 1, :], D), ALU.mult))
            chain(dve.tensor_tensor(t1[:, :, :], t1[:, :, :], each(rowb[:, 0, :], W), ALU.add))
            chain(dve.tensor_tensor(t1[:, :, :], t1[:, :, :], x[:, :, :], ALU.add))
            norm(chain, x, False, LAYERS + 2)
            barrier(dve, "L1")

            for n in range(2):
                dve.memset(nmax, FAR)
                chain(dve.memset(acc, 0.0))
                for r in range(U):
                    copy_idx(r, r)
                dve.wait_ge(conv_loaded, 128 * (n + 1))
                for k, (a, b) in enumerate(CHUNKS):
                    if k >= 2:
                        dve.wait_ge(kvs_stored[k % 2], 16 * (n * len(CHUNKS[k % 2::2]) + k // 2))
                    for w in range(a, b):
                        ps = pAB[w % 2]
                        dve.wait_ge(c_down, n * W + w + 1)
                        dve.tensor_tensor(q[:, w, :], ps[:, 0:HC], bcat[:, 0:HC], ALU.add)
                        last = dve.tensor_tensor(kvs[:, k % 2, w - a, :], ps[:, HC:3 * HC], bcat[:, HC:3 * HC], ALU.add)
                        if w == b - 1:
                            last.then_inc(kvs_ready, 1)
                        dve.tensor_tensor(skip[:, w, :], ps[:, 3 * HC:QKVS], bcat[:, 3 * HC:QKVS], ALU.add).then_inc(c_used, 1)

                def turned_hot(t, r, half):
                    dve.wait_ge(dbc_loaded[r], t * 16 + (16 + half * TRIPS * 16))
                    return dve.tensor_scalar(ohT[:, r % 2, :], dbc[:, r, :], iotap[:, 0:1], None, ALU.is_equal)

                def maximum(t, r):
                    at = t * U + (r + n * NI)
                    dve.wait_ge(al_spread, at + 1)
                    dve.wait_ge(far_ready, at + 1)
                    hold(dve)
                    for kh in range(4):
                        part = pspread[:, kh * 256:(kh + 1) * 256]
                        last = dve.tensor_tensor_reduce(out=part, in0=part, in1=far[:, r % 2, (kh // 2) * 256:(kh // 2 + 1) * 256],
                                                        scale=1.0, scalar=FAR, op0=ALU.add, op1=ALU.max, accum_out=gmax[:, r % 2, kh:kh + 1])
                    last.then_inc(c_chain, 1)
                    dve.wait_ge(c_chain, at * 3 + 1)
                    for k in range(2):
                        w = dve.value_load(win[0:1, bass.ds((t * U + r) * 2 + k, 1)], min_val=0, max_val=W - 1)
                        own = nmax[:, bass.ds(w * HEADS, HEADS)]
                        dve.tensor_tensor(own, own, gmax[:, r % 2, 2 * k:2 * k + 2], ALU.max).then_inc(c_chain, 1)
                        dve.wait_ge(c_chain, at * 3 + (2 + k))

                def score(t, r, first, last):
                    at = t * U + (r + 1 + n * NI)
                    dve.wait_ge(gathered[r], t * 64 + (64 + SCORES[n] * TRIPS * 64))
                    dve.wait_ge(q_ready, at)
                    dve.tensor_tensor(prod.rearrange("p (c h) f -> p c (h f)", h=HEADS),
                                      pacc[:, (r % 2) * 512:(r % 2 + 1) * 512].rearrange("p (c f) -> p c f", c=4),
                                      kv[:, r, :, 0:HC], ALU.mult).then_inc(e_chain, 1)
                    dve.wait_ge(e_chain, at + LAYERS * NI)
                    dve.tensor_reduce(al[:, r % 2, :], prod, AX_X, ALU.add).then_inc(al_ready, 1)
                    copy_idx(t * U + (r + U), r)
                    if not (first and r == 0):
                        dve.wait_ge(far_ready, at - 1)
                    if not last:
                        if r == U - 1:
                            turned_hot(t + 1, 0, 2 * n).then_inc(ohT_ready, 1)
                        else:
                            turned_hot(t, r + 1, 2 * n).then_inc(ohT_ready, 1)
                    if not (first and r == 0):
                        maximum(t, r - 1)

                turned_hot(0, 0, 2 * n).then_inc(ohT_ready, 1)
                for r in range(U):
                    score(0, r, True, False)
                with dve.Fori(1, TRIPS - 1) as t:
                    for r in range(U):
                        score(t, r, False, False)
                for r in range(U):
                    score(TRIPS - 1, r, False, r == U - 1)
                maximum(TRIPS - 1, U - 1)
                barrier(dve, f"scores{n}")

                def add_sums(t, r):
                    at = t * U + (r + n * NI)
                    dve.wait_ge(sums_ready, at + 1)
                    for k in range(2):
                        w = dve.value_load(win[0:1, bass.ds((t * U + r) * 2 + k, 1)], min_val=0, max_val=W - 1)
                        own = flat(acc)[:, bass.ds(w * AW, AW)]
                        dve.tensor_tensor(own, own, pAB[r % 2][:, k * AW:(k + 1) * AW], ALU.add).then_inc(b_chain, 1)
                        dve.wait_ge(b_chain, at * 2 + (1 + k))

                def weigh(t, r, first):
                    at = t * U + (r + 1 + n * NI)
                    turned_hot(t, r, 2 * n + 1).then_inc(ohT_ready, 1)
                    one_hot(t * U + r, r)
                    if not (first and r == 0):
                        add_sums(t, r - 1)
                    dve.wait_ge(m_ready, at)
                    dve.tensor_tensor(dif[:, r % 2, :].rearrange("p (c h) -> p c h", h=HEADS),
                                      alpha[:, bass.ds((t * U + r) * 8, 8)].rearrange("p (c h) -> p c h", h=HEADS),
                                      pacc[:, (r % 2) * 512:(r % 2) * 512 + 4 * NPAD].rearrange("p (c m) -> p c m", c=4)[:, :, 0:HEADS],
                                      ALU.subtract).then_inc(dif_ready, 1)
                    dve.wait_ge(ex_ready, at)
                    dve.wait_ge(v_loaded[r], t * 16 + (16 + n * TRIPS * 16))
                    dve.tensor_copy(vm[:, r % 2, :, HC:AW], ex[:, r % 2, :].rearrange("p (c h) -> p c h", h=HEADS))
                    dve.tensor_tensor(vm[:, r % 2, :, 0:HC].rearrange("p c (h f) -> p c h f", h=HEADS),
                                      vbuf[:, r, :].rearrange("p (c h f) -> p c h f", c=4, h=HEADS),
                                      ex[:, r % 2, :].rearrange("p (c h) -> p c h", h=HEADS).unsqueeze(3).to_broadcast([P, 4, HEADS, D]),
                                      ALU.mult).then_inc(vm_ready, 1)

                for r in range(U):
                    weigh(0, r, True)
                with dve.Fori(1, TRIPS) as t:
                    for r in range(U):
                        weigh(t, r, False)
                add_sums(TRIPS - 1, U - 1)
                barrier(dve, f"sums{n}")

                chain(dve.tensor_scalar(den, acc[:, :, HC:AW], 1e-16, None, ALU.add))
                chain(dve.reciprocal(den, den))
                chain(dve.tensor_scalar(den, den, 1.0 / HEADS, None, ALU.mult))
                chain(dve.tensor_tensor(t1[:, :, :], acc[:, :, 0:D], over(den[:, :, 0], D), ALU.mult))
                chain(dve.tensor_tensor(t2[:, :, :], acc[:, :, D:HC], over(den[:, :, 1], D), ALU.mult))
                chain(dve.tensor_tensor(t1[:, :, :], t1[:, :, :], t2[:, :, :], ALU.add))
                if n == 0:
                    chain(dve.tensor_tensor(x0[:, :, :], t1[:, :, :], skip, ALU.add))
                else:
                    chain(dve.tensor_tensor(t1[:, :, :], t1[:, :, :], skip, ALU.add))
                    chain(dve.tensor_tensor(t1[:, :, :], t1[:, :, :], x[:, :, :], ALU.add))
                    norm(chain, x, False, LAYERS + 3)
                barrier(dve, f"conv{n}")

            for r in range(U):
                copy_idx(r, r)
            with dve.Fori(0, TRIPS) as t:
                for r in range(U):
                    dve.wait_ge(scattered, t * U + ((LAYERS + 1) * NI + r + 1))
                    one_hot(t * U + r, r)
                    dve.wait_ge(a_loaded[r], t * 32 + 32)
                    dve.wait_ge(gathered[r], t * 64 + ((LAYERS + 3) * TRIPS * 64 + 64))
                    dve.tensor_tensor(sum3[:, r % 2, :, :], a64[:, r, :, :], g[:, r, :, :], ALU.add).then_inc(sum_ready, 1)
                    copy_idx(t * U + (r + U), r)
            dve.wait_ge(summed, LAYERS + 2)
            chain(dve.tensor_tensor(flat(t1[:, :, :]), sums, flat(x[:, :, :]), ALU.add))
            chain(dve.tensor_tensor(t1[:, :, :], t1[:, :, :], x[:, :, :], ALU.add))
            norm(chain, x, False, LAYERS + 4)
            dve.drain().then_inc(final_ready, 1)


_CONV = [f"L2_gnn_l{l}_{a}{b}" for l in (1, 2) for b in "qkvs" for a in "wb"]
_INS = ["x", "src", "dst", "edge_attr_32", "edge_attr_64"] + [
    f"L0_gnn_{k}" for k in ("W1", "b1", "W2", "b2", "We1", "be1", "We2", "be2", "res_w", "dot_scale", "ln_g", "ln_b")
] + ["L1_gnn_weight", "L1_gnn_bias"] + _CONV


def kernel(**inputs):
    import numpy as np
    import concourse.bacc as bacc
    from concourse.bass_utils import run_bass_kernel_spmd

    nc = bacc.Bacc("TRN2", target_bir_lowering=False, num_devices=1)
    arrays, args = {}, []
    for name in _INS:
        a = np.ascontiguousarray(inputs[name])
        arrays[f"in_{name}"] = a
        args.append(nc.dram_tensor(f"in_{name}", a.shape, mybir.dt.from_np(a.dtype), kind="ExternalInput").ap())
    out = nc.dram_tensor("out_0", (N, D), F32, kind="ExternalOutput").ap()
    k = len(args) - len(_CONV)
    graph_kernel(nc, *args[:k], args[k:], out)
    r = run_bass_kernel_spmd(nc, [arrays], core_ids=[0])
    return r.results[0]["out_0"]
```

```python
from contextlib import ExitStack

import concourse.bass as bass
from concourse import mybir

ALU = mybir.AluOpType
ACT = mybir.ActivationFunctionType
F32 = mybir.dt.float32
BF16 = mybir.dt.bfloat16
I32 = mybir.dt.int32
U32 = mybir.dt.uint32
AX_X = mybir.AxisListType.X

P = 128
N = 3125
D = 64
E = 100000
DA = 32
LAYERS = 5
HEADS = 2
W = -(-N // P)
NP = W * P
TAIL = N - (W - 1) * P
EP = 125
ET = E // EP
GROUP = 2 * P
NG = -(-(E // GROUP + W) // 8) * 8
SLOTS = NG * GROUP
NB = 2 * NG
NI = NG // 2
U = 4
TRIPS = NI // U
UB = 4 * U
ROW = D + DA + 2
SRC_AT, DST_AT = D + DA, D + DA + 1
ST = 10
S_STEPS = ET // ST
IDX = NI + U
LAGS = (-1, 0, 1, 3)
CH = 4
CHUNKS = [(a, min(a + CH, W)) for a in range(0, W, CH)]
NCH = len(CHUNKS)
HC = HEADS * D
AW = HC + HEADS
QKVS = 3 * HC + D
PARTS = 3
PARTS_W = W * HEADS * PARTS
LN_EPS = 1e-5
FAR = -1e30
FILL = 32
BIGW = (NI + 1) * P


class Chain:

    def __init__(self, eng, sem, base=0):
        self.eng, self.sem, self.base, self.n = eng, sem, base, 0

    def __call__(self, ins):
        self.n += 1
        ins.then_inc(self.sem, 1)
        self.eng.wait_ge(self.sem, self.base + self.n)


def graph_kernel(nc, x_in, src_in, dst_in, a32_in, a64_in, w1_in, b1_in, w2_in, b2_in, we1_in, be1_in,
                 we2_in, be2_in, resw_in, dots_in, lng_in, lnb_in, gw_in, gb_in, conv_in, out):
    with ExitStack() as ctx:
        def sb(name, shape, dt=F32):
            return ctx.enter_context(nc.sbuf_tensor(name, shape, dt))

        def sem(name):
            return ctx.enter_context(nc.semaphore(name))

        def dram(name, shape, dt=F32):
            return nc.dram_tensor(name, shape, dt, kind="Internal").ap()

        rows = dram("rows", (SLOTS, ROW))
        htab = dram("htab", (NP, D))
        kvtab = dram("kvtab", (NP, 2 * HC))
        vslot = dram("vslot", (NI, P, 4 * HC))
        dstT = dram("dstT", (NB, P), BF16)

        big = sb("big", [P, BIGW])
        x = sb("x", [P, W, D])
        x0 = sb("x0", [P, W, D])
        work = sb("work", [P, 2, W, D])
        t1, t2 = work[:, 0, :, :], work[:, 1, :, :]
        tab = sb("tab", [P, W, D])
        xT = sb("xT", [D, NP])
        srcidx = sb("srcidx", [P, NB + 4 * U], U32)
        dstl = sb("dstl", [P, NB])
        idx = sb("idx", [P, U, 4], U32)
        g = sb("g", [P, U, 4, D])
        oh = sb("oh", [P, 2, 4, P])
        msg = sb("msg", [P, 2, 4, D])
        eb = sb("eb", [P, 4, D])
        hb = sb("hb", [P, 2, 512])
        hid = sb("hid", [P, 2, 512])
        iota = sb("iota", [P, P])
        iotap = sb("iotap", [P, 1])
        ident = sb("ident", [P, P])
        zero = sb("zero", [P, 512])
        win = sb("win", [1, len(LAGS), NG + 2 * U], I32)
        deg = sb("deg", [P, 2, W])
        st = sb("st", [P, 8, W])
        w1 = sb("w1", [D, 2 * D])
        w2 = sb("w2", [2 * D, D])
        we1 = sb("we1", [P, 2, P])
        we2 = sb("we2", [P, P])
        cols = sb("cols", [P, 4])
        scale = sb("scale", [P, 1])
        rowb = sb("rowb", [P, 4, D])

        def carver():
            at = [0]

            def carve(*shape, dt=F32):
                n = 1
                for s in shape:
                    n *= s
                words = n // 2 if dt == BF16 else n
                v = big[:, at[0]:at[0] + words]
                at[0] += words
                assert at[0] <= BIGW
                if dt != F32:
                    v = v.bitcast(dt)
                if len(shape) == 2:
                    v = v.rearrange("p (a b) -> p a b", a=shape[0])
                if len(shape) == 3:
                    v = v.rearrange("p (a b c) -> p a b c", a=shape[0], b=shape[1])
                return v
            return carve

        carve = carver()
        src_i = carve(ET, dt=I32)
        dst_i = carve(ET, dt=I32)
        tmp_i = carve(ET, dt=I32)
        key = carve(4, ET)
        mask = carve(ET)
        scan = carve(ET)
        zrow = carve(ET)
        slotf = carve(ET)
        slot = carve(ET, dt=U32)
        cnt = carve(W)
        base = carve(W)
        grp = carve(3, W)
        grp_i = carve(W, dt=I32)
        wid = carve(W)
        tri = carve(P)
        ones = carve(P)
        gio = carve(NG)
        gacc = carve(NG)
        fill = carve(FILL * ROW)
        stage = carve(2, ST, ROW)
        sidx = carve(2, ST, dt=U32)
        low = [[carve(ST, P, dt=BF16) for _ in range(2)] for _ in range(2)]
        high = [[carve(ST, W + 1, dt=BF16) for _ in range(2)] for _ in range(2)]

        carve = carver()
        q = carve(W, HC)
        skip = carve(W, D)
        acc = carve(W, AW)
        kv = carve(U, 4, 2 * HC)
        ohT = carve(2, 512)
        ohTb = carve(2, 512, dt=BF16)
        far = carve(U, 512)
        prod = carve(8, D)
        al = carve(U, 8)
        alpha = carve(NI * 8)
        alT = carve(2, P)
        pick = carve(8, P)
        dbc = carve(U, 512, dt=BF16)
        gmax = carve(2, 4)
        nmax = carve(W * HEADS)
        rest = carve(W * HEADS)
        parts = carve(PARTS_W, dt=BF16)
        wcat = carve(QKVS)
        bcat = carve(QKVS)
        vbuf = carve(U, 4 * HC)
        vm = carve(2, 4, AW)
        msum = carve(2, 8)
        dif = carve(2, 8)
        den = carve(W, HEADS)
        away = far.rearrange("p (u c) (k m) -> p u (c k) m", u=2, k=4)[:, :, 0:4, :]
        kvs = vbuf.rearrange("p u (c f) -> p (u c) f", c=2).rearrange("p (k w) f -> p k w f", k=2)

        carve = carver()
        a64 = carve(U, 4, D)
        sum3 = carve(2, 4, D)

        rowst = work[:, :, :, :].rearrange("p k w f -> p (k w f)")[:, 0:2 * UB * ROW].rearrange("p (u c r) -> p u c r", u=2, c=UB)
        turned = tab[:, :, :].rearrange("p w f -> p (w f)").bitcast(BF16)

        pacc = ctx.enter_context(nc.psum_tensor("pacc", [P, 2048], F32))
        pA = ctx.enter_context(nc.psum_tensor("pA", [P, 512], F32))
        pB = ctx.enter_context(nc.psum_tensor("pB", [P, 512], F32))
        pC = ctx.enter_context(nc.psum_tensor("pC", [P, 512], F32))
        pD = ctx.enter_context(nc.psum_tensor("pD", [P, 512], F32))
        pT = [pC, pD]
        pAB = [pA, pB]
        pspread = [pacc[:, 0:1024], pacc[:, 1024:2048]]

        ended = sem("ended")
        const_ready = sem("const_ready")
        p_chain = sem("p_chain")
        x_loaded = sem("x_loaded")
        ids_loaded = sem("ids_loaded")
        filled = sem("filled")
        v_chain = sem("v_chain")
        w_chain = sem("w_chain")
        s_chain = sem("s_chain")
        counted = sem("counted")
        crossed = sem("crossed")
        stage_loaded = [sem(f"stage_loaded{r}") for r in range(2)]
        stage_ready = sem("stage_ready")
        degree_used = sem("degree_used")
        rows_sent = [sem(f"rows_sent{r}") for r in range(2)]
        row_loaded = [sem(f"row_loaded{r}") for r in range(2)]
        row_split = sem("row_split")
        row_turned = sem("row_turned")
        row_kept = sem("row_kept")
        dst_turned = sem("dst_turned")
        dst_copied = sem("dst_copied")
        dst_stored = sem("dst_stored")
        weights = sem("weights")
        w_free = sem("w_free")
        x_ready = sem("x_ready")
        n_turned = sem("n_turned")
        n_copied = sem("n_copied")
        n_up = sem("n_up")
        n_biased = sem("n_biased")
        n_act = sem("n_act")
        n_down = sem("n_down")
        tab_ready = sem("tab_ready")
        tab_stored = sem("tab_stored")
        idx_ready = sem("idx_ready")
        gathered = [sem(f"gathered{r}") for r in range(U)]
        e_up = sem("e_up")
        e_biased = sem("e_biased")
        e_act = sem("e_act")
        e_down = sem("e_down")
        e_chain = sem("e_chain")
        l_chain = sem("l_chain")
        msg_ready = sem("msg_ready")
        scattered = sem("scattered")
        summed = sem("summed")
        conv_loaded = sem("conv_loaded")
        c_down = sem("c_down")
        c_used = sem("c_used")
        kvs_ready = sem("kvs_ready")
        kvs_stored = [sem(f"kvs_stored{r}") for r in range(2)]
        dbc_loaded = [sem(f"dbc_loaded{r}") for r in range(U)]
        ohT_ready = sem("ohT_ready")
        far_ready = sem("far_ready")
        q_ready = sem("q_ready")
        n_chain = sem("n_chain")
        max_taken = sem("max_taken")
        b_chain = sem("b_chain")
        m_added = sem("m_added")
        al_ready = sem("al_ready")
        al_turned = sem("al_turned")
        al_copied = sem("al_copied")
        al_spread = sem("al_spread")
        v_stored = [sem(f"v_stored{r}") for r in range(U)]
        v_loaded = [sem(f"v_loaded{r}") for r in range(U)]
        parts_ready = sem("parts_ready")
        m_ready = sem("m_ready")
        dif_ready = sem("dif_ready")
        ex_ready = sem("ex_ready")
        away_ready = sem("away_ready")
        hot_ready = sem("hot_ready")
        vm_ready = sem("vm_ready")
        sums_ready = sem("sums_ready")
        a_loaded = [sem(f"a_loaded{r}") for r in range(U)]
        sum_ready = sem("sum_ready")
        deg_ready = sem("deg_ready")
        var_ready = sem("var_ready")
        root_ready = sem("root_ready")
        final_ready = sem("final_ready")
        stored = sem("stored")

        block = ctx.enter_context(nc.Block())
        PHASES = ["sorted", "unpacked", "L0", "L1", "scores0", "sums0", "conv0", "scores1", "sums1", "conv1"]

        def barrier(eng, name):
            eng.drain().then_inc(ended, 1)
            eng.wait_ge(ended, 5 * (PHASES.index(name) + 1))

        def back(t, r, k):
            return (t, r - k) if r >= k else (t - 1, r - k + U)

        def ahead(t, r, k):
            return (t, r + k) if r + k < U else (t + 1, r + k - U)

        def windows(engine, t, lag):
            _, v = nc.values_load_multi_w_load_instructions(
                win[0:1, LAGS.index(lag), bass.ds(t * (2 * U), 2 * U)], engines=(engine,), min_val=0, max_val=W - 1)
            return lambda r, k: v[2 * r + k]

        PE, DVE = mybir.EngineType.PE, mybir.EngineType.DVE

        def hold(eng):
            eng.nop(nofuse=True)

        def nodes(t):
            return t.rearrange("(w p) f -> p w f", p=P)

        def flat(t):
            return t.rearrange("p w f -> p (w f)")

        def row_of(v, w):
            return v.rearrange("(o f) -> o f", o=1).to_broadcast([P, w])

        conv = [conv_in[0:8], conv_in[8:16]]
        WEIGHT_DMAS = 16 + 1
        TURNS = [(a, min(a + P, NB)) for a in range(0, NB, P)]
        SCORES = [LAYERS + 1, LAYERS + 2]

        @block.sync
        def _(sp):
            sp.dma_start(src_i[0:EP, :], src_in.rearrange("(p t) -> p t", p=EP)).then_inc(ids_loaded, 16)
            sp.dma_start(dst_i[0:EP, :], dst_in.rearrange("(p t) -> p t", p=EP)).then_inc(ids_loaded, 16)
            sp.wait_ge(const_ready, 1)
            sp.dma_start(x[:, 0:W - 1, :], nodes(x_in[0:(W - 1) * P, :])).then_inc(x_loaded, 16)
            sp.dma_start(x[0:TAIL, W - 1, :], x_in[(W - 1) * P:N, :]).then_inc(x_loaded, 16)
            rows_f = rows.rearrange("(p a r) c -> p a (r c)", p=P, r=FILL)
            with sp.Fori(0, SLOTS // P // FILL) as a:
                sp.dma_start(rows_f[:, bass.ds(a, 1), :].rearrange("p o c -> p (o c)"), fill).then_inc(filled, 16)

            a64_v = a64_in.rearrange("(p t) f -> p t f", p=EP)
            a32_v = a32_in.rearrange("(p t) f -> p t f", p=EP)

            def load_stage(t, r):
                i = t * 2 + r
                sp.dma_start(stage[0:EP, r, :, 0:D], a64_v[:, bass.ds(i * ST, ST), :]).then_inc(stage_loaded[r], 16)
                sp.dma_start(stage[0:EP, r, :, D:D + DA], a32_v[:, bass.ds(i * ST, ST), :]).then_inc(stage_loaded[r], 16)

            for r in range(2):
                load_stage(0, r)
            with sp.Fori(1, S_STEPS // 2) as t:
                for r in range(2):
                    sp.wait_ge(rows_sent[r], t * (16 * ST))
                    load_stage(t, r)
            for r in range(2):
                sp.wait_ge(rows_sent[r], S_STEPS // 2 * 16 * ST)
            barrier(sp, "sorted")

            rows_v = rows.rearrange("(g p b) r -> p g (b r)", p=P, b=2)

            def load_rows(t, r):
                sp.dma_start(rowst[:, r, :, :].rearrange("p (g b) r -> p g (b r)", b=2),
                             rows_v[:, bass.ds((t * 2 + r) * (2 * U), 2 * U), :]).then_inc(row_loaded[r], 16)

            for r in range(2):
                load_rows(0, r)
            with sp.Fori(1, TRIPS // 2) as t:
                for r in range(2):
                    sp.wait_ge(row_split, t * 2 + (r - 1))
                    load_rows(t, r)
            for k, (a, b) in enumerate(TURNS):
                sp.wait_ge(dst_copied, k + 1)
                sp.dma_start(dstT[a:b, :], turned[0:b - a, k * P:(k + 1) * P]).then_inc(dst_stored, 16)
            sp.wait_ge(dst_stored, 16 * len(TURNS))
            barrier(sp, "unpacked")

            with sp.Fori(0, LAYERS) as l:
                def layer(v):
                    v = v[bass.ds(l, 1)]
                    return v.rearrange("o a b -> (o a) b") if len(v.shape) == 3 else v

                sp.wait_ge(w_free, l + 1)
                sp.dma_start(w1[:, :], layer(w1_in)).then_inc(weights, 16)
                sp.dma_start(w2[:, :], layer(w2_in)).then_inc(weights, 16)
                for c in range(4):
                    sp.dma_start(we1[c * DA:(c + 1) * DA, c // 2, (c % 2) * D:(c % 2 + 1) * D], layer(we1_in)).then_inc(weights, 16)
                for c in range(2):
                    sp.dma_start(we2[c * D:(c + 1) * D, c * D:(c + 1) * D], layer(we2_in)).then_inc(weights, 16)
                    sp.dma_start(cols[c * D:(c + 1) * D, 1:2], layer(be1_in).rearrange("o (a u) -> (o a) u", u=1)).then_inc(weights, 16)
                sp.dma_start(cols[:, 0:1], layer(b1_in).rearrange("o (a u) -> (o a) u", u=1)).then_inc(weights, 16)
                for k, v in enumerate((resw_in, dots_in)):
                    sp.dma_start(cols[:, 2 + k:3 + k], layer(v).rearrange("(o u) -> o u", u=1).to_broadcast([P, 1])).then_inc(weights, 16)
                for k, v in enumerate((b2_in, be2_in, lng_in, lnb_in)):
                    sp.dma_start(rowb[:, k, :], layer(v).to_broadcast([P, D])).then_inc(weights, 16)
                sp.wait_ge(tab_ready, l * NCH + NCH)
                sp.dma_start(nodes(htab), tab[:, :, :]).then_inc(tab_stored, 16)
            barrier(sp, "L0")

            sp.dma_start(w1[:, 0:D], gw_in).then_inc(weights, 16)
            sp.dma_start(rowb[:, 0, :], row_of(gb_in, D)).then_inc(weights, 16)
            sp.wait_ge(tab_ready, (LAYERS + 1) * NCH)
            sp.dma_start(nodes(htab), tab[:, :, :]).then_inc(tab_stored, 16)
            barrier(sp, "L1")

            dst_v = dstT.rearrange("(i c) p -> i (c p)", c=4)

            def load_dst(t, r):
                sp.dma_start(dbc[:, r, :], dst_v[bass.ds(t * U + r, 1), :].to_broadcast([P, 512])).then_inc(dbc_loaded[r], 16)

            for n in range(2):
                for k in range(4):
                    w = HC if k < 3 else D
                    sp.dma_start(wcat[0:D, k * HC:k * HC + w], conv[n][2 * k]).then_inc(conv_loaded, 16)
                    sp.dma_start(bcat[:, k * HC:k * HC + w], row_of(conv[n][2 * k + 1], w)).then_inc(conv_loaded, 16)
                for k, (a, b) in enumerate(CHUNKS):
                    sp.wait_ge(kvs_ready, n * NCH + k + 1)
                    sp.dma_start(nodes(kvtab)[:, a:b, :], kvs[:, k % 2, 0:b - a, :]).then_inc(kvs_stored[k % 2], 16)

                def store_v(t, r):
                    sp.wait_ge(gathered[r], (t + SCORES[n] * TRIPS) * 64 + 64)
                    sp.dma_start(vslot[bass.ds(t * U + r, 1)].rearrange("i p (c f) -> (i p) c f", c=4),
                                 kv[:, r, :, HC:2 * HC]).then_inc(v_stored[r], 16)

                for r in range(U):
                    load_dst(0, r)
                with sp.Fori(1, TRIPS) as t:
                    for r in range(U):
                        sp.wait_ge(ohT_ready, t * U + (r + 1 - U + 2 * n * NI))
                        load_dst(t, r)
                        store_v(t - 1, r)
                for r in range(U):
                    store_v(TRIPS - 1, r)
                for r in range(U):
                    sp.wait_ge(v_stored[r], (n + 1) * TRIPS * 16)
                barrier(sp, f"scores{n}")

                def load_v(t, r):
                    sp.dma_start(vbuf[:, r, :], vslot[bass.ds(t * U + r, 1)].rearrange("i p f -> (i p) f")).then_inc(v_loaded[r], 16)

                for r in range(U):
                    load_dst(0, r)
                    load_v(0, r)
                with sp.Fori(1, TRIPS) as t:
                    for r in range(U):
                        sp.wait_ge(ohT_ready, t * U + (r + 1 - U + (2 * n + 1) * NI))
                        load_dst(t, r)
                        sp.wait_ge(vm_ready, t * U + (r + 1 - U + n * NI))
                        load_v(t, r)
                barrier(sp, f"sums{n}")
                barrier(sp, f"conv{n}")

            sp.dma_start(nodes(htab), x[:, :, :]).then_inc(tab_stored, 16)

            rows_b = rows.rearrange("(i k p b) r -> i p k b r", k=2, p=P, b=2)

            def load_a(t, r):
                for k in range(2):
                    sp.dma_start(a64[:, r, 2 * k:2 * k + 2, :],
                                 rows_b[bass.ds(t * U + r, 1), :, k, :, 0:D].rearrange("i p b r -> (i p) b r")).then_inc(a_loaded[r], 16)

            for r in range(U):
                load_a(0, r)
            with sp.Fori(1, TRIPS) as t:
                for r in range(U):
                    sp.wait_ge(sum_ready, t * U + (r + 1 - U))
                    load_a(t, r)
            sp.wait_ge(final_ready, 1)
            sp.dma_start(nodes(out[0:(W - 1) * P, :]), x[:, 0:W - 1, :]).then_inc(stored, 16)
            sp.dma_start(out[(W - 1) * P:N, :], x[0:TAIL, W - 1, :]).then_inc(stored, 16)
            sp.wait_ge(stored, 32)

        @block.gpsimd
        def _(pool):
            chain = Chain(pool, p_chain)
            pool.memset(x[:, W - 1, :], 0.0)
            chain(pool.memset(fill, 0.0))
            chain(pool.memset(fill.rearrange("p (r c) -> p r c", c=ROW)[:, :, DST_AT:DST_AT + 1], -1.0))
            pool.memset(zero[:, :], 0.0)
            pool.memset(ones, 1.0)
            pool.memset(we1[:, :, :], 0.0)
            pool.memset(we2[:, :], 0.0)
            pool.memset(ident[:, :], 0.0)
            chain(pool.memset(tri, 1.0))
            pool.iota(iota[:, :], pattern=[[1, P]], base=0, channel_multiplier=0, allow_small_or_imprecise_dtypes=True)
            pool.iota(iotap[:, :], pattern=[[0, 1]], base=0, channel_multiplier=1, allow_small_or_imprecise_dtypes=True)
            pool.iota(wid, pattern=[[1, W]], base=0, channel_multiplier=0, allow_small_or_imprecise_dtypes=True)
            pool.iota(gio, pattern=[[1, NG]], base=0, channel_multiplier=0, allow_small_or_imprecise_dtypes=True)
            pool.affine_select(out=ident[:, :], in_=ident[:, :], compare_op=ALU.not_equal, fill=1.0, base=0,
                               pattern=[[-1, P]], channel_multiplier=1)
            chain(pool.affine_select(out=tri, in_=tri, compare_op=ALU.is_gt, fill=0.0, base=0,
                                     pattern=[[1, P]], channel_multiplier=-1))
            pool.drain().then_inc(const_ready, 1)
            pool.wait_ge(filled, SLOTS // P // FILL * 16)

            with pool.Fori(0, S_STEPS // 2) as t:
                for r in range(2):
                    pool.wait_ge(stage_loaded[r], t * 32 + 32)
                    pool.wait_ge(stage_ready, t * 2 + (r + 1))
                    hold(pool)
                    for c in range(ST):
                        pool.indirect_dma_start(
                            out=rows[:, :], out_offset=bass.IndirectOffsetOnAxis(ap=sidx[0:EP, r, c:c + 1], axis=0),
                            in_=stage[0:EP, r, c, :], in_offset=None).then_inc(rows_sent[r], 16)
            barrier(pool, "sorted")
            barrier(pool, "unpacked")

            def gather(table, into, r):
                for c in range(4):
                    pool.indirect_dma_start(
                        out=into[:, r, c, :], out_offset=None, in_=table[:, :],
                        in_offset=bass.IndirectOffsetOnAxis(ap=idx[:, r, c:c + 1], axis=0)).then_inc(gathered[r], 16)

            with pool.Fori(0, LAYERS) as l:
                pool.wait_ge(tab_stored, l * 16 + 16)
                hold(pool)
                with pool.Fori(0, TRIPS) as t:
                    for r in range(U):
                        pool.wait_ge(idx_ready, l * IDX + t * U + (r + 1))
                        hold(pool)
                        gather(htab, g, r)
            barrier(pool, "L0")

            pool.wait_ge(tab_stored, LAYERS * 16 + 16)
            with pool.Fori(0, TRIPS) as t:
                for r in range(U):
                    pool.wait_ge(idx_ready, t * U + (LAYERS * IDX + r + 1))
                    pool.wait_ge(scattered, t * U + (LAYERS * NI + 2 + r + 1 - U))
                    hold(pool)
                    gather(htab, g, r)
            barrier(pool, "L1")

            pool.memset(alT, 0.0)
            chain(pool.memset(pick, 0.0))
            pool.affine_select(out=pick, in_=pick, compare_op=ALU.not_equal, fill=1.0, base=0,
                               pattern=[[-1, 8], [0, P]], channel_multiplier=1)
            pool.drain().then_inc(const_ready, 1)
            for n in range(2):
                for k in range(2):
                    pool.wait_ge(kvs_stored[k], 16 * (n + 1) * len(CHUNKS[k::2]))

                def step(t, r, first):
                    pool.wait_ge(idx_ready, t * U + (SCORES[n] * IDX + r + 1))
                    if not first:
                        pool.wait_ge(v_stored[r], t * 16 + n * TRIPS * 16)
                    hold(pool)
                    gather(kvtab, kv, r)

                for r in range(U):
                    step(0, r, True)
                with pool.Fori(1, TRIPS) as t:
                    for r in range(U):
                        step(t, r, False)
                barrier(pool, f"scores{n}")
                barrier(pool, f"sums{n}")
                barrier(pool, f"conv{n}")

            pool.wait_ge(tab_stored, (LAYERS + 2) * 16)
            with pool.Fori(0, TRIPS) as t:
                for r in range(U):
                    pool.wait_ge(idx_ready, t * U + ((LAYERS + 3) * IDX + r + 1))
                    hold(pool)
                    gather(htab, g, r)

        @block.scalar
        def _(act):
            act.drain().then_inc(row_kept, 2)

            def root(nth):
                act.wait_ge(var_ready, nth)
                act.activation(st[:, 4, :], st[:, 3, :], ACT.Sqrt).then_inc(root_ready, 1)

            act.wait_ge(deg_ready, 1)
            act.activation(deg[:, :, :], deg[:, :, :], ACT.Sqrt).then_inc(deg_ready, 1)
            barrier(act, "sorted")
            with act.Fori(0, TRIPS // 2) as t:
                for r in range(2):
                    act.wait_ge(row_turned, t * 2 + (r + 1))
                    act.copy(big[:, bass.ds((t * 2 + r) * (U * P), U * P)], pT[r][:, :]).then_inc(row_kept, 1)
            for k, (a, b) in enumerate(TURNS):
                act.wait_ge(dst_turned, k + 1)
                act.copy(turned[0:b - a, k * P:(k + 1) * P], pT[k % 2][0:b - a, 0:P]).then_inc(dst_copied, 1)
            barrier(act, "unpacked")

            def copy_turned(first):
                for k, (a, b) in enumerate(CHUNKS):
                    act.wait_ge(n_turned, first + (k + 1))
                    act.copy(xT[:, a * P:b * P], pT[k % 2][0:D, 0:(b - a) * P]).then_inc(n_copied, 1)

            with act.Fori(0, LAYERS) as l:
                copy_turned(l * NCH)
                act.wait_ge(weights, l * (16 * WEIGHT_DMAS) + 16 * WEIGHT_DMAS)
                for k, (a, b) in enumerate(CHUNKS):
                    act.wait_ge(n_up, l * NCH + (k + 1))
                    n = (b - a) * P
                    act.activation(hb[:, k % 2, 0:n], pacc[:, (k % 2) * 512:(k % 2) * 512 + n], ACT.Identity, bias=cols[:, 0:1]).then_inc(n_biased, 1)
                with act.Fori(0, TRIPS) as t:
                    for r in range(U):
                        act.wait_ge(e_up, l * (NI + 1) + t * U + (r + 1))
                        act.activation(hb[:, 0, 0:2 * P], pA[:, 0:2 * P], ACT.Identity, bias=cols[:, 1:2]).then_inc(e_biased, 1)
                root(l + 1)
            root(LAYERS + 1)
            barrier(act, "L0")
            copy_turned(LAYERS * NCH)
            root(LAYERS + 2)
            barrier(act, "L1")
            act.wait_ge(const_ready, 2)
            for n in range(2):
                copy_turned((LAYERS + 1 + n) * NCH)

                def far_of(t, r):
                    act.wait_ge(ohT_ready, t * U + (r + 1 + 2 * n * NI))
                    act.activation(far[:, r, :], ohT[:, r % 2, :], ACT.Copy, scale=-FAR, bias=FAR).then_inc(far_ready, 1)

                def step(t, r, last):
                    act.wait_ge(al_ready, t * U + (r + 1 + n * NI))
                    act.copy(alpha[:, bass.ds((t * U + r) * 8, 8)], al[:, r, :])
                    act.wait_ge(al_turned, t * U + (r + 1 + n * NI))
                    act.copy(alT[0:8, r % 2, :], pT[r % 2][0:8, 0:P]).then_inc(al_copied, 1)
                    if not (last and r == U - 1):
                        far_of(*ahead(t, r, 1))

                far_of(0, 0)
                with act.Fori(0, TRIPS - 1) as t:
                    for r in range(U):
                        step(t, r, False)
                for r in range(U):
                    step(TRIPS - 1, r, True)
                barrier(act, f"scores{n}")
                def trip(t, first):
                    for r in range(U):
                        act.wait_ge(dif_ready, t * U + (r + 1 + n * NI))
                        act.activation(vm[:, r % 2, :, HC:AW], dif[:, r % 2, :].rearrange("p (c h) -> p c h", h=HEADS), ACT.Exp, scale=float(D) ** -0.5).then_inc(ex_ready, 1)
                        if not (first and r < 2):
                            act.wait_ge(sums_ready, t * U + (r - 1 + n * NI))
                        for c in range(4):
                            last = act.activation(away[:, r % 2, c, :], iota[:, :], ACT.Abs, scale=-1.0,
                                                  bias=dstl[:, bass.ds((t * U + r) * 4 + c, 1)])
                        last.then_inc(away_ready, 1)
                        act.wait_ge(away_ready, t * U + (r + 1 + n * NI))
                        act.activation(oh[:, r % 2, :, :], away[:, r % 2, :, :], ACT.Relu, scale=-1.0, bias=1.0).then_inc(hot_ready, 1)

                trip(0, True)
                with act.Fori(1, TRIPS) as t:
                    trip(t, False)
                barrier(act, f"sums{n}")
                if n == 1:
                    root(LAYERS + 3)
                barrier(act, f"conv{n}")
            with act.Fori(0, TRIPS) as t:
                for r in range(U):
                    act.wait_ge(sum_ready, t * U + (r + 1))
                    act.activation(msg[:, r % 2, :, :], sum3[:, r % 2, :, :], ACT.Relu).then_inc(msg_ready, 1)
            root(LAYERS + 4)

        @block.tensor
        def _(pe):
            pe.wait_ge(const_ready, 1)
            pe.wait_ge(counted, 1)
            pe.matmul(pA[:, 0:W], tri[0:EP, :], cnt[0:EP, :], start=True, stop=True)
            pe.matmul(pB[:, 0:W], ones[0:EP, :], cnt[0:EP, :], start=True, stop=True).then_inc(crossed, 1)
            for k in range(2):
                pe.matmul(pT[k][:, 0:W], zero[:, 0:P], zero[:, 0:W], start=True, stop=False, skip_group_check=True)
            with pe.Fori(0, S_STEPS // 2) as t:
                for r in range(2):
                    pe.wait_ge(stage_ready, t * 2 + (r + 1))
                    for k in range(2):
                        for c in range(ST):
                            last = pe.matmul(pT[k][:, 0:W], low[r][k][0:EP, c, :], high[r][k][0:EP, c, 0:W],
                                             start=False, stop=False, skip_group_check=True)
                    last.then_inc(degree_used, 1)
            barrier(pe, "sorted")
            with pe.Fori(0, TRIPS // 2) as t:
                for r in range(2):
                    pe.wait_ge(row_split, t * 2 + (r + 1))
                    pe.wait_ge(row_kept, t * 2 + (r + 1))
                    for j in range(U):
                        last = pe.transpose(pT[r][:, j * P:(j + 1) * P], hb[:, r, j * P:(j + 1) * P], ident[:, :])
                    last.then_inc(row_turned, 1)
            pe.wait_ge(row_kept, TRIPS + 2)
            for k, (a, b) in enumerate(TURNS):
                if k >= 2:
                    pe.wait_ge(dst_copied, k - 1)
                pe.transpose(pT[k % 2][0:b - a, 0:P], dstl[:, a:b], ident[:, :]).then_inc(dst_turned, 1)
            pe.drain().then_inc(scattered, 2)
            barrier(pe, "unpacked")

            def turn(src, first):
                for k, (a, b) in enumerate(CHUNKS):
                    if k >= 2:
                        pe.wait_ge(n_copied, first + (k - 1))
                    hold(pe)
                    for w in range(a, b):
                        last = pe.transpose(pT[k % 2][0:D, (w - a) * P:(w - a + 1) * P], src[:, w, :], ident[:, :])
                    last.then_inc(n_turned, 1)

            def open_sums():
                for b in range(4):
                    pe.matmul(pacc[:, b * 512:(b + 1) * 512], zero[:, 0:P], zero[:, :], start=True, stop=False, skip_group_check=True)

            def scatter(at, r, rows_of):
                for k in range(2):
                    w = at(k)
                    for b in range(2):
                        c = 2 * k + b
                        last = pe.matmul(pacc[:, bass.ds(w * D, D)], oh[:, r % 2, c, :], rows_of(r, c),
                                         start=False, stop=False, skip_group_check=True)
                last.then_inc(scattered, 1)

            def up(i):
                for k in range(2):
                    last = pe.matmul(pA[:, k * P:(k + 1) * P], we1[:, k, :], big[:, bass.ds(i * P, P)], start=True, stop=True)
                last.then_inc(e_up, 1)

            with pe.Fori(0, LAYERS) as l:
                pe.wait_ge(x_ready, l + 1)
                turn(x, l * NCH)
                pe.wait_ge(weights, l * (16 * WEIGHT_DMAS) + 16 * WEIGHT_DMAS)

                def node_up(k):
                    a, b = CHUNKS[k]
                    pe.wait_ge(n_copied, l * NCH + (k + 1))
                    pe.matmul(pacc[:, (k % 2) * 512:(k % 2) * 512 + (b - a) * P], w1[:, :], xT[:, a * P:b * P], start=True, stop=True).then_inc(n_up, 1)

                node_up(0)
                for k, (a, b) in enumerate(CHUNKS):
                    if k + 1 < NCH:
                        node_up(k + 1)
                    pe.wait_ge(n_act, l * NCH + (k + 1))
                    for w in range(b - a):
                        last = pe.matmul(pAB[k % 2][:, w * D:(w + 1) * D], hid[:, k % 2, w * P:(w + 1) * P], w2[:, :], start=True, stop=True)
                    last.then_inc(n_down, 1)
                open_sums()
                pe.wait_ge(tab_ready, l * NCH + NCH)
                def message(r, c):
                    return msg[:, r % 2, c, :]

                def trip(t, first):
                    w = windows(PE, t, 1)
                    for r in range(U):
                        pe.wait_ge(e_act, l * NI + t * U + (r + 1))
                        for k in range(2):
                            last = pe.matmul(pB[:, k * P:(k + 1) * P], hid[:, 0, k * P:(k + 1) * P], we2[:, :], start=True, stop=True)
                        last.then_inc(e_down, 1)
                        up(t * U + (r + 1))
                        if not (first and r == 0):
                            tb, rb = back(t, r, 1)
                            pe.wait_ge(msg_ready, l * NI + tb * U + (rb + 1))
                            scatter(lambda k: w(r, k), rb, message)

                up(0)
                trip(0, True)
                with pe.Fori(1, TRIPS) as t:
                    trip(t, False)
                w = windows(PE, TRIPS, 1)
                pe.wait_ge(msg_ready, l * NI + NI)
                scatter(lambda k: w(0, k), U - 1, message)
                pe.drain().then_inc(summed, 1)
            barrier(pe, "L0")

            pe.wait_ge(x_ready, LAYERS + 2)
            turn(t2, LAYERS * NCH)
            open_sums()
            pe.wait_ge(weights, LAYERS * 16 * WEIGHT_DMAS + 32)
            for k, (a, b) in enumerate(CHUNKS):
                pe.wait_ge(n_copied, LAYERS * NCH + k + 1)
                if k:
                    pe.wait_ge(tab_ready, LAYERS * NCH + k)
                for w in range(a, b):
                    last = pe.matmul(pB[:, (w - a) * D:(w - a + 1) * D], xT[:, w * P:(w + 1) * P], w1[:, 0:D], start=True, stop=True)
                last.then_inc(n_down, 1)
            with pe.Fori(0, TRIPS) as t:
                w = windows(PE, t, 0)
                for r in range(U):
                    pe.wait_ge(gathered[r], t * 64 + (LAYERS * TRIPS * 64 + 64))
                    pe.wait_ge(msg_ready, t * U + (LAYERS * NI + r + 1))
                    scatter(lambda k: w(r, k), r, lambda r, c: g[:, r, c, :])
            pe.drain().then_inc(summed, 1)
            barrier(pe, "L1")

            pe.wait_ge(const_ready, 2)
            for n in range(2):
                turn((x, x0)[n], (LAYERS + 1 + n) * NCH)
                pe.wait_ge(conv_loaded, 128 * (n + 1))
                for k, (a, b) in enumerate(CHUNKS):
                    pe.wait_ge(n_copied, (LAYERS + 1 + n) * NCH + k + 1)
                    for w in range(a, b):
                        if w >= 2:
                            pe.wait_ge(c_used, n * W + w - 1)
                        pe.matmul(pAB[w % 2][:, 0:QKVS], xT[:, w * P:(w + 1) * P], wcat[0:D, :], start=True, stop=True).then_inc(c_down, 1)
                pe.wait_ge(c_used, (n + 1) * W)

                def spread(t, r, first):
                    at = t * U + (r + n * NI)
                    pe.wait_ge(al_copied, at + 1)
                    if not (first and r < 2):
                        pe.wait_ge(max_taken, at - 1)
                    for c in range(4):
                        for h in range(HEADS):
                            col = ((c // 2) * 4 + h * 2 + c % 2) * P
                            last = pe.matmul(pspread[r % 2][:, col:col + P], pick[:, 2 * c + h, :], alT[:, r % 2, :], start=True, stop=True)
                    last.then_inc(al_spread, 1)

                def step(t, r, at, first):
                    pe.wait_ge(ohT_ready, t * U + (r + 1 + 2 * n * NI))
                    for k in range(2):
                        w = at(r, k)
                        for b in range(2):
                            c = 2 * k + b
                            last = pe.matmul(pAB[r % 2][:, c * P:(c + 1) * P],
                                             ohT[:, r % 2, c * P:(c + 1) * P], flat(q)[:, bass.ds(w * HC, HC)], start=True, stop=True)
                    last.then_inc(q_ready, 1)
                    if not (first and r == 0):
                        spread(*back(t, r, 1), first)
                    pe.wait_ge(al_ready, t * U + (r + 1 + n * NI))
                    pe.transpose(pT[r % 2][0:8, 0:P], al[:, r, :], ident[:, :]).then_inc(al_turned, 1)

                w = windows(PE, 0, 0)
                for r in range(U):
                    step(0, r, w, True)
                with pe.Fori(1, TRIPS) as t:
                    w = windows(PE, t, 0)
                    for r in range(U):
                        step(t, r, w, False)
                spread(TRIPS - 1, U - 1, False)
                barrier(pe, f"scores{n}")

                def maxima(t, r, at):
                    pe.wait_ge(ohT_ready, t * U + (r + 1 + (2 * n + 1) * NI))
                    for k in range(2):
                        w = at(k)
                        for b in range(2):
                            c = 2 * k + b
                            m = HEADS * PARTS
                            last = pe.matmul(pT[r % 2][:, c * m:(c + 1) * m], ohTb[:, r % 2, c * P:(c + 1) * P],
                                             parts[:, bass.ds(w * m, m)], start=True, stop=True)
                    last.then_inc(m_ready, 1)

                def step(t, r, at, last_trip):
                    if not (last_trip and r == U - 1):
                        maxima(*ahead(t, r, 1), lambda k: at(r, k))
                    pe.wait_ge(vm_ready, t * U + (r + 1 + n * NI))
                    pe.wait_ge(hot_ready, t * U + (r + 1 + n * NI))
                    for c in range(4):
                        last = pe.matmul(pAB[r % 2][:, (c // 2) * AW:(c // 2 + 1) * AW], oh[:, r % 2, c, :],
                                         vm[:, r % 2, c, :], start=(c % 2 == 0), stop=(c % 2 == 1))
                    last.then_inc(sums_ready, 1)

                pe.wait_ge(parts_ready, n + 1)
                w = windows(PE, 0, 0)
                maxima(0, 0, lambda k: w(0, k))
                with pe.Fori(0, TRIPS - 1) as t:
                    w = windows(PE, t, -1)
                    for r in range(U):
                        step(t, r, w, False)
                w = windows(PE, TRIPS - 1, -1)
                for r in range(U):
                    step(TRIPS - 1, r, w, True)
                barrier(pe, f"sums{n}")
                barrier(pe, f"conv{n}")

            open_sums()
            with pe.Fori(0, TRIPS) as t:
                w = windows(PE, t, 0)
                for r in range(U):
                    pe.wait_ge(msg_ready, t * U + ((LAYERS + 1) * NI + r + 1))
                    scatter(lambda k: w(r, k), r, lambda r, c: msg[:, r % 2, c, :])
            pe.drain().then_inc(summed, 1)

        @block.vector
        def _(dve):
            chain = Chain(dve, v_chain)

            def over(v, n):
                return v.unsqueeze(2).to_broadcast([v.shape[0], v.shape[1], n])

            def each(v, n):
                return v.unsqueeze(1).to_broadcast([v.shape[0], n, v.shape[1]])

            dve.wait_ge(const_ready, 1)
            dve.wait_ge(ids_loaded, 32)
            for k, ids in enumerate((src_i, dst_i)):
                chain(dve.tensor_scalar(tmp_i[0:EP, :], ids[0:EP, :], P - 1, None, ALU.bitwise_and))
                chain(dve.tensor_copy(key[0:EP, 2 * k, :], tmp_i[0:EP, :]))
                chain(dve.tensor_scalar(tmp_i[0:EP, :], ids[0:EP, :], P.bit_length() - 1, None, ALU.logical_shift_right))
                chain(dve.tensor_copy(key[0:EP, 2 * k + 1, :], tmp_i[0:EP, :]))
            dve.memset(zrow, 0.0)
            chain(dve.memset(gacc, 0.0))

            with dve.Fori(0, W) as w:
                wc = Chain(dve, w_chain, w)
                wc(dve.tensor_scalar(mask[0:EP, :], key[0:EP, 3, :], wid[0:EP, bass.ds(w, 1)], 0.0, ALU.is_equal, ALU.add,
                                     accum_out=cnt[0:EP, bass.ds(w, 1)]))
            dve.drain().then_inc(counted, 1)
            dve.wait_ge(crossed, 1)
            chain(dve.tensor_scalar(grp[:, 0, :], pB[:, 0:W], float(GROUP - 1), None, ALU.add))
            chain(dve.tensor_copy(grp_i, grp[:, 0, :]))
            chain(dve.tensor_scalar(grp_i, grp_i, GROUP.bit_length() - 1, None, ALU.logical_shift_right))
            chain(dve.tensor_copy(grp[:, 0, :], grp_i))
            chain(dve.tensor_tensor_scan(grp[:, 1, :], grp[:, 0, :], zrow[:, 0:W], 0.0, ALU.add, ALU.add))
            chain(dve.tensor_tensor(grp[:, 2, :], grp[:, 1, :], grp[:, 0, :], ALU.subtract))
            chain(dve.scalar_tensor_tensor(base, grp[:, 2, :], float(GROUP), pA[:, 0:W], ALU.mult, ALU.add))
            chain(dve.tensor_scalar(base, base, -1.0, None, ALU.add))
            with dve.Fori(0, W) as w:
                sc = Chain(dve, s_chain, w * 4)
                sc(dve.tensor_scalar(mask[0:EP, :], key[0:EP, 3, :], wid[0:EP, bass.ds(w, 1)], None, ALU.is_equal))
                sc(dve.tensor_tensor_scan(scan[0:EP, :], mask[0:EP, :], zrow[0:EP, :], base[0:EP, bass.ds(w, 1)], ALU.add, ALU.add))
                hold(dve)
                sc(dve.copy_predicated(slotf[0:EP, :], mask[0:EP, :].bitcast(U32), scan[0:EP, :]))
                sc(dve.scalar_tensor_tensor(gacc, gio, grp[:, 1, bass.ds(w, 1)], gacc, ALU.is_ge, ALU.add))
            chain(dve.tensor_copy(slot[0:EP, :], slotf[0:EP, :]))
            chain(dve.tensor_scalar(gacc, gacc, float(W - 1), None, ALU.min))
            chain(dve.memset(win[0:1, :, :], 0))
            for k, lag in enumerate(LAGS):
                a = max(0, -2 * lag)
                chain(dve.tensor_copy(win[0:1, k, a + 2 * lag:NG + 2 * lag], gacc[0:1, a:NG]))

            stage_i = stage.bitcast(I32)

            def stage_step(t, r, first):
                i = t * 2 + r
                if not first:
                    dve.wait_ge(rows_sent[r], t * (16 * ST))
                    dve.wait_ge(degree_used, t * 2 + (r - 1))
                dve.tensor_copy(sidx[0:EP, r, :], slot[0:EP, bass.ds(i * ST, ST)])
                dve.tensor_copy(stage_i[0:EP, r, :, SRC_AT], src_i[0:EP, bass.ds(i * ST, ST)])
                dve.tensor_copy(stage[0:EP, r, :, DST_AT], key[0:EP, 2, bass.ds(i * ST, ST)])
                for k in range(2):
                    dve.tensor_tensor(low[r][k][0:EP, :, :], each(iota[0:EP, :], ST), over(key[0:EP, 2 * k, bass.ds(i * ST, ST)], P), ALU.is_equal)
                    last = dve.tensor_tensor(high[r][k][0:EP, :, 0:W], each(wid[0:EP, :], ST),
                                             over(key[0:EP, 2 * k + 1, bass.ds(i * ST, ST)], W), ALU.is_equal)
                last.then_inc(stage_ready, 1)

            for r in range(2):
                stage_step(0, r, True)
            with dve.Fori(1, S_STEPS // 2) as t:
                for r in range(2):
                    stage_step(t, r, False)
            dve.wait_ge(degree_used, S_STEPS)
            for k in range(2):
                last = dve.tensor_scalar(deg[:, k, :], pT[k][:, 0:W], 1.0, None, ALU.max)
            last.then_inc(deg_ready, 1)
            dve.wait_ge(deg_ready, 2)
            chain(dve.reciprocal(deg[:, :, :], deg[:, :, :]))
            barrier(dve, "sorted")

            chain(dve.memset(srcidx[:, NB:], 0))
            rowst_u = rowst.bitcast(U32)

            def take_apart(t, r, first):
                dve.wait_ge(row_loaded[r], t * 16 + 16)
                if not first:
                    dve.wait_ge(row_turned, t * 2 + (r - 1))
                dve.tensor_copy(hb[:, r, :].rearrange("p (c f) -> p c f", c=UB), rowst[:, r, :, D:D + DA])
                dve.tensor_copy(srcidx[:, bass.ds((t * 2 + r) * UB, UB)], rowst_u[:, r, :, SRC_AT])
                dve.tensor_copy(dstl[:, bass.ds((t * 2 + r) * UB, UB)], rowst[:, r, :, DST_AT]).then_inc(row_split, 1)

            for r in range(2):
                take_apart(0, r, True)
            with dve.Fori(1, TRIPS // 2) as t:
                for r in range(2):
                    take_apart(t, r, False)
            dve.memset(big[:, NI * P:], 0.0)
            dve.wait_ge(x_loaded, 32)
            chain(dve.tensor_copy(x0[:, :, :], x[:, :, :]))
            barrier(dve, "unpacked")

            def copy_idx(i, r):
                dve.tensor_copy(idx[:, r, :], srcidx[:, bass.ds(i * 4, 4)]).then_inc(idx_ready, 1)

            def one_hot(i, r):
                return dve.tensor_tensor(oh[:, r % 2, :, :], each(iota[:, :], 4), over(dstl[:, bass.ds(i * 4, 4)], P), ALU.is_equal)

            def norm(ch, dst, affine, nth):
                ch(dve.tensor_reduce(st[:, 0, :], t1, AX_X, ALU.add))
                ch(dve.tensor_scalar(st[:, 1, :], st[:, 0, :], 1.0 / D, None, ALU.mult))
                ch(dve.tensor_tensor(t1, t1, over(st[:, 1, :], D), ALU.subtract))
                ch(dve.tensor_tensor(t2, t1, t1, ALU.mult))
                ch(dve.tensor_reduce(st[:, 2, :], t2, AX_X, ALU.add))
                dve.tensor_scalar(st[:, 3, :], st[:, 2, :], 1.0 / D, LN_EPS, ALU.mult, ALU.add).then_inc(var_ready, 1)
                dve.wait_ge(root_ready, nth)
                ch(dve.reciprocal(st[:, 5, :], st[:, 4, :]))
                ch(dve.tensor_tensor(dst[:, :, :], t1, over(st[:, 5, :], D), ALU.mult))
                if affine:
                    ch(dve.tensor_tensor(dst[:, :, :], dst[:, :, :], each(rowb[:, 2, :], W), ALU.mult))
                    ch(dve.tensor_tensor(dst[:, :, :], dst[:, :, :], each(rowb[:, 3, :], W), ALU.add))

            sums = pacc[:, 0:W * D]

            dve.drain().then_inc(x_ready, 1)
            dve.drain().then_inc(w_free, 1)
            END = 11
            with dve.Fori(0, LAYERS) as l:
                dve.wait_ge(weights, l * (16 * WEIGHT_DMAS) + 16 * WEIGHT_DMAS)

                def node_act(k):
                    n = (CHUNKS[k][1] - CHUNKS[k][0]) * P
                    dve.wait_ge(n_biased, l * NCH + (k + 1))
                    dve.scalar_tensor_tensor(hid[:, k % 2, 0:n], hb[:, k % 2, 0:n], 0.1, hb[:, k % 2, 0:n], ALU.mult, ALU.max).then_inc(n_act, 1)

                node_act(0)
                for k, (a, b) in enumerate(CHUNKS):
                    if k + 1 < NCH:
                        node_act(k + 1)
                    dve.wait_ge(n_down, l * NCH + (k + 1))
                    dve.tensor_tensor(tab[:, a:b, :], pAB[k % 2][:, 0:(b - a) * D].rearrange("p (w f) -> p w f", w=b - a),
                                      each(rowb[:, 0, :], b - a), ALU.add).then_inc(tab_ready, 1)
                for r in range(U):
                    copy_idx(r, r)
                with dve.Fori(0, TRIPS) as t:
                    for r in range(U):
                        i = t * U + r
                        dve.wait_ge(e_biased, l * NI + t * U + (r + 1))
                        dve.scalar_tensor_tensor(hid[:, 0, 0:2 * P], hb[:, 0, 0:2 * P], 0.1, hb[:, 0, 0:2 * P], ALU.mult, ALU.max).then_inc(e_act, 1)
                        dve.wait_ge(scattered, l * NI + t * U + (r + 1))
                        one_hot(i, r)
                        dve.wait_ge(e_down, l * NI + t * U + (r + 1))
                        dve.tensor_tensor(eb[:, :, :], pB[:, 0:4 * D].rearrange("p (c f) -> p c f", c=4), each(rowb[:, 1, :], 4), ALU.add).then_inc(e_chain, 1)
                        dve.wait_ge(gathered[r], l * (TRIPS * 64) + t * 64 + 64)
                        dve.wait_ge(e_chain, l * NI + t * U + (r + 1))
                        dve.tensor_tensor(msg[:, r % 2, :, :], eb[:, :, :], g[:, r, :, :], ALU.mult).then_inc(msg_ready, 1)
                        copy_idx(i + U, r)
                lc = Chain(dve, l_chain, l * END)
                lc(dve.tensor_tensor(scale[:, :], cols[:, 2:3], cols[:, 3:4], ALU.mult))
                dve.wait_ge(summed, l + 1)
                lc(dve.scalar_tensor_tensor(flat(t1), sums, scale[:, 0:1], flat(x[:, :, :]), ALU.mult, ALU.add))
                norm(lc, x, True, l + 1)
                assert lc.n == END
                hold(dve)
                dve.drain().then_inc(x_ready, 1)
                dve.drain().then_inc(w_free, 1)
            chain(dve.tensor_tensor(t1, x0[:, :, :], x[:, :, :], ALU.add))
            norm(chain, x, False, LAYERS + 1)
            barrier(dve, "L0")

            chain(dve.tensor_tensor(t2, x[:, :, :], over(deg[:, 0, :], D), ALU.mult))
            dve.drain().then_inc(x_ready, 1)
            for r in range(U):
                copy_idx(r, r)
            for k, (a, b) in enumerate(CHUNKS):
                dve.wait_ge(n_down, LAYERS * NCH + k + 1)
                dve.tensor_copy(flat(tab[:, a:b, :]), pB[:, 0:(b - a) * D]).then_inc(tab_ready, 1)
            with dve.Fori(0, TRIPS) as t:
                for r in range(U):
                    dve.wait_ge(scattered, t * U + (LAYERS * NI + r + 1))
                    one_hot(t * U + r, r).then_inc(msg_ready, 1)
                    dve.wait_ge(gathered[r], t * 64 + (LAYERS * TRIPS * 64 + 64))
                    copy_idx(t * U + (r + U), r)
            dve.wait_ge(summed, LAYERS + 1)
            dve.wait_ge(weights, LAYERS * 16 * WEIGHT_DMAS + 32)
            chain(dve.tensor_tensor(t1, sums.rearrange("p (w f) -> p w f", w=W), over(deg[:, 1, :], D), ALU.mult))
            chain(dve.tensor_tensor(t1, t1, each(rowb[:, 0, :], W), ALU.add))
            chain(dve.tensor_tensor(t1, t1, x[:, :, :], ALU.add))
            norm(chain, x, False, LAYERS + 2)
            barrier(dve, "L1")

            for n in range(2):
                dve.memset(nmax, FAR)
                chain(dve.memset(acc, 0.0))
                for r in range(U):
                    copy_idx(r, r)
                dve.wait_ge(conv_loaded, 128 * (n + 1))
                for k, (a, b) in enumerate(CHUNKS):
                    if k >= 2:
                        dve.wait_ge(kvs_stored[k % 2], 16 * (n * len(CHUNKS[k % 2::2]) + k // 2))
                    for w in range(a, b):
                        ps = pAB[w % 2]
                        dve.wait_ge(c_down, n * W + w + 1)
                        dve.tensor_tensor(q[:, w, :], ps[:, 0:HC], bcat[:, 0:HC], ALU.add)
                        last = dve.tensor_tensor(kvs[:, k % 2, w - a, :], ps[:, HC:3 * HC], bcat[:, HC:3 * HC], ALU.add)
                        if w == b - 1:
                            last.then_inc(kvs_ready, 1)
                        dve.tensor_tensor(skip[:, w, :], ps[:, 3 * HC:QKVS], bcat[:, 3 * HC:QKVS], ALU.add).then_inc(c_used, 1)

                def turned_hot(to, t, r, nth):
                    dve.wait_ge(dbc_loaded[r], t * 16 + (16 + nth * TRIPS * 16))
                    dve.tensor_scalar(to[:, r % 2, :], dbc[:, r, :], iotap[:, 0:1], None, ALU.is_equal).then_inc(ohT_ready, 1)

                def maximum(t, r):
                    at = t * U + (r + n * NI)
                    dve.wait_ge(al_spread, at + 1)
                    dve.wait_ge(far_ready, at + 1)
                    hold(dve)
                    for kh in range(4):
                        part = pspread[r % 2][:, kh * 256:(kh + 1) * 256]
                        last = dve.tensor_tensor_reduce(out=part, in0=part, in1=far[:, r, (kh // 2) * 256:(kh // 2 + 1) * 256],
                                                        scale=1.0, scalar=FAR, op0=ALU.add, op1=ALU.max, accum_out=gmax[:, r % 2, kh:kh + 1])
                    last.then_inc(max_taken, 1)

                def keep_max(t, r, k, w):
                    at = t * U + (r + n * NI)
                    own = nmax[:, bass.ds(w * HEADS, HEADS)]
                    dve.wait_ge(max_taken, at + 1)
                    if not (isinstance(at, int) and at + k == 0):
                        dve.wait_ge(n_chain, at * 2 + k)
                    dve.tensor_tensor(own, own, gmax[:, r % 2, 2 * k:2 * k + 2], ALU.max).then_inc(n_chain, 1)

                def score(t, r, w, first, last):
                    at = t * U + (r + 1 + n * NI)
                    dve.wait_ge(gathered[r], t * 64 + (64 + SCORES[n] * TRIPS * 64))
                    dve.wait_ge(q_ready, at)
                    dve.tensor_tensor(prod.rearrange("p (c h) f -> p c (h f)", h=HEADS),
                                      pAB[r % 2][:, :].rearrange("p (c f) -> p c f", c=4),
                                      kv[:, r, :, 0:HC], ALU.mult).then_inc(e_chain, 1)
                    if not (first and r < 3):
                        keep_max(*back(t, r, 3), 0, w(r, 0))
                    dve.wait_ge(e_chain, at + LAYERS * NI)
                    dve.tensor_reduce(al[:, r, :], prod, AX_X, ALU.add).then_inc(al_ready, 1)
                    copy_idx(t * U + (r + U), r)
                    if not (first and r < 3):
                        keep_max(*back(t, r, 3), 1, w(r, 1))
                    if not (last and r == U - 1):
                        if not (first and r == 0):
                            dve.wait_ge(far_ready, at - 1)
                        turned_hot(ohT, *ahead(t, r, 1), 2 * n)
                    if not (first and r < 2):
                        maximum(*back(t, r, 2))

                turned_hot(ohT, 0, 0, 2 * n)
                w = windows(DVE, 0, 3)
                for r in range(U):
                    score(0, r, w, True, False)
                with dve.Fori(1, TRIPS - 1) as t:
                    w = windows(DVE, t, 3)
                    for r in range(U):
                        score(t, r, w, False, False)
                w = windows(DVE, TRIPS - 1, 3)
                for r in range(U):
                    score(TRIPS - 1, r, w, False, r == U - 1)
                w = windows(DVE, TRIPS, 3)
                for r in range(3):
                    for k in range(2):
                        keep_max(TRIPS - 1, r + 1, k, w(r, k))
                    if r < 2:
                        maximum(TRIPS - 1, r + 2)
                dve.wait_ge(n_chain, (n + 1) * NI * 2)
                pv = parts.rearrange("p (m j) -> p m j", j=PARTS)
                chain(dve.tensor_copy(pv[:, :, 0], nmax))
                chain(dve.tensor_tensor(rest, nmax, pv[:, :, 0], ALU.subtract))
                chain(dve.tensor_copy(pv[:, :, 1], rest))
                chain(dve.tensor_tensor(pv[:, :, 2], rest, pv[:, :, 1], ALU.subtract))
                dve.drain().then_inc(parts_ready, 1)
                barrier(dve, f"scores{n}")

                def add_sums(t, r, k, w):
                    at = t * U + (r + n * NI)
                    own = flat(acc)[:, bass.ds(w * AW, AW)]
                    dve.wait_ge(sums_ready, at + 1)
                    if not (isinstance(at, int) and at + k == 0):
                        dve.wait_ge(b_chain, at * 2 + k)
                    dve.tensor_tensor(own, own, pAB[r % 2][:, k * AW:(k + 1) * AW], ALU.add).then_inc(b_chain, 1)

                def add_parts(t, r):
                    dve.wait_ge(m_ready, t * U + (r + 1 + n * NI))
                    dve.tensor_reduce(msum[:, r % 2, :], pT[r % 2][:, 0:8 * PARTS].rearrange("p (m j) -> p m j", j=PARTS),
                                      AX_X, ALU.add).then_inc(m_added, 1)

                def differ(t, r):
                    dve.wait_ge(m_added, t * U + (r + 1 + n * NI))
                    dve.tensor_tensor(dif[:, r % 2, :], alpha[:, bass.ds((t * U + r) * 8, 8)], msum[:, r % 2, :],
                                      ALU.subtract).then_inc(dif_ready, 1)

                def weigh(t, r, w, first, last):
                    dve.wait_ge(ex_ready, t * U + (r + 1 + n * NI))
                    dve.wait_ge(v_loaded[r], t * 16 + (16 + n * TRIPS * 16))
                    dve.tensor_tensor(vm[:, r % 2, :, 0:HC].rearrange("p c (h f) -> p c h f", h=HEADS),
                                      vbuf[:, r, :].rearrange("p (c h f) -> p c h f", c=4, h=HEADS),
                                      vm[:, r % 2, :, HC:AW].unsqueeze(3).to_broadcast([P, 4, HEADS, D]),
                                      ALU.mult).then_inc(vm_ready, 1)
                    if not (last and r == U - 1):
                        add_parts(*ahead(t, r, 1))
                    if not (first and r == 0):
                        add_sums(*back(t, r, 1), 0, w(r, 0))
                    if not (last and r == U - 1):
                        differ(*ahead(t, r, 1))
                    if not (first and r == 0):
                        add_sums(*back(t, r, 1), 1, w(r, 1))
                    if not (last and r >= U - 2):
                        turned_hot(ohTb, *ahead(t, r, 2), 2 * n + 1)

                turned_hot(ohTb, 0, 0, 2 * n + 1)
                turned_hot(ohTb, 0, 1, 2 * n + 1)
                add_parts(0, 0)
                differ(0, 0)
                w = windows(DVE, 0, 1)
                for r in range(U):
                    weigh(0, r, w, True, False)
                with dve.Fori(1, TRIPS - 1) as t:
                    w = windows(DVE, t, 1)
                    for r in range(U):
                        weigh(t, r, w, False, False)
                w = windows(DVE, TRIPS - 1, 1)
                for r in range(U):
                    weigh(TRIPS - 1, r, w, False, True)
                w = windows(DVE, TRIPS, 1)
                for k in range(2):
                    add_sums(TRIPS - 1, U - 1, k, w(0, k))
                barrier(dve, f"sums{n}")

                chain(dve.tensor_scalar(den, acc[:, :, HC:AW], 1e-16, None, ALU.add))
                chain(dve.reciprocal(den, den))
                chain(dve.tensor_scalar(den, den, 1.0 / HEADS, None, ALU.mult))
                chain(dve.tensor_tensor(t1, acc[:, :, 0:D], over(den[:, :, 0], D), ALU.mult))
                chain(dve.tensor_tensor(t2, acc[:, :, D:HC], over(den[:, :, 1], D), ALU.mult))
                chain(dve.tensor_tensor(t1, t1, t2, ALU.add))
                if n == 0:
                    chain(dve.tensor_tensor(x0[:, :, :], t1, skip, ALU.add))
                else:
                    chain(dve.tensor_tensor(t1, t1, skip, ALU.add))
                    chain(dve.tensor_tensor(t1, t1, x[:, :, :], ALU.add))
                    norm(chain, x, False, LAYERS + 3)
                barrier(dve, f"conv{n}")

            for r in range(U):
                copy_idx(r, r)
            with dve.Fori(0, TRIPS) as t:
                for r in range(U):
                    dve.wait_ge(scattered, t * U + ((LAYERS + 1) * NI + r + 1))
                    one_hot(t * U + r, r)
                    dve.wait_ge(a_loaded[r], t * 32 + 32)
                    dve.wait_ge(gathered[r], t * 64 + ((LAYERS + 3) * TRIPS * 64 + 64))
                    dve.tensor_tensor(sum3[:, r % 2, :, :], a64[:, r, :, :], g[:, r, :, :], ALU.add).then_inc(sum_ready, 1)
                    copy_idx(t * U + (r + U), r)
            dve.wait_ge(summed, LAYERS + 2)
            chain(dve.tensor_tensor(flat(t1), sums, flat(x[:, :, :]), ALU.add))
            chain(dve.tensor_tensor(t1, t1, x[:, :, :], ALU.add))
            norm(chain, x, False, LAYERS + 4)
            dve.drain().then_inc(final_ready, 1)


_CONV = [f"L2_gnn_l{l}_{a}{b}" for l in (1, 2) for b in "qkvs" for a in "wb"]
_INS = ["x", "src", "dst", "edge_attr_32", "edge_attr_64"] + [
    f"L0_gnn_{k}" for k in ("W1", "b1", "W2", "b2", "We1", "be1", "We2", "be2", "res_w", "dot_scale", "ln_g", "ln_b")
] + ["L1_gnn_weight", "L1_gnn_bias"] + _CONV


def kernel(**inputs):
    import numpy as np
    import concourse.bacc as bacc
    from concourse.bass_utils import run_bass_kernel_spmd

    nc = bacc.Bacc("TRN2", target_bir_lowering=False, num_devices=1)
    arrays, args = {}, []
    for name in _INS:
        a = np.ascontiguousarray(inputs[name])
        arrays[f"in_{name}"] = a
        args.append(nc.dram_tensor(f"in_{name}", a.shape, mybir.dt.from_np(a.dtype), kind="ExternalInput").ap())
    out = nc.dram_tensor("out_0", (N, D), F32, kind="ExternalOutput").ap()
    k = len(args) - len(_CONV)
    graph_kernel(nc, *args[:k], args[k:], out)
    r = run_bass_kernel_spmd(nc, [arrays], core_ids=[0])
    return r.results[0]["out_0"]
```
